# Optimizing a Trainium2 kernel written in Bass

```python
import numpy as np
import jax
import jax.numpy as jnp

def _softmax(x, axis=-1):
    return jax.nn.softmax(x, axis=axis)

def _gelu(x):
    return jax.nn.gelu(x, approximate=True)

def _silu(x):
    return jax.nn.silu(x)

def _sigmoid(x):
    return jax.nn.sigmoid(x)

def _layernorm(x, axis=-1, eps=1e-05):
    m = jnp.mean(x, axis=axis, keepdims=True)
    v = jnp.var(x, axis=axis, keepdims=True)
    return (x - m) / jnp.sqrt(v + eps)

def _scatter_add(tgt, idx, src, axis=0):
    return tgt.at[idx].add(src)

def _segment_sum(src, seg, n):
    return jax.ops.segment_sum(src, seg, n)
kernel_name = 'mk_perceiver_d1_seqx_r8_c08834'

def setup_inputs(seed: int=0):
    np.random.seed(seed)
    _w = jnp.asarray

    def _rec_inputs():
        import jax
        import jax.numpy as jnp
        _rk = jax.random.key(seed)
        x = -0.000929 + 1 * jax.random.normal(jax.random.fold_in(_rk, 1), (32, 64, 128), jnp.float32)
        _lenS = 64 - jax.random.randint(jax.random.fold_in(_rk, 7), (32,), 0, max(1, 64 // 4) + 1, jnp.int32)
        _lenS2 = 128 - jax.random.randint(jax.random.fold_in(_rk, 8), (32,), 0, max(1, 128 // 4) + 1, jnp.int32)
        _ctx_1024P = jax.random.normal(jax.random.fold_in(_rk, 11), (32, 16, 128), jnp.float32)
        _ctx_1024c = jax.random.dirichlet(jax.random.fold_in(_rk, 511), 0.3 * jnp.ones((16,), jnp.float32), (32, 128))
        _ctx_1024t = jnp.einsum('bsk,bkd->bsd', _ctx_1024c, _ctx_1024P)
        _ctx_1024t = _ctx_1024t * jax.lax.rsqrt(jnp.mean(jnp.square(_ctx_1024t)) + 1e-12) * 0.953939
        ctx_1024 = -1.52775e-05 + 0.999936 * (_ctx_1024t + 0.3 * jax.random.normal(jax.random.fold_in(_rk, 611), (32, 128, 128), jnp.float32))
        return (x, ctx_1024)
    x, ctx_1024 = _rec_inputs()

    def _L0_xattn_setup():
        import jax, jax.numpy as jnp
        import numpy as np
        DIM = 128
        H = 16
        D = 64
        INNER = H * D
        EPS = 1e-05

        def layernorm(x, w, b):
            mu = jnp.mean(x, axis=-1, keepdims=True)
            var = jnp.var(x, axis=-1, keepdims=True)
            return (x - mu) * jax.lax.rsqrt(var + EPS) * w + b
        key = jax.random.key(seed)
        ks = jax.random.split(key, 8)
        B, N, S = (4, 32, 1024)
        s = 1.0 / np.sqrt(DIM)
        return {'latents': jax.random.normal(ks[0], (B, N, DIM), jnp.float32), 'context': jax.random.normal(ks[1], (B, S, DIM), jnp.float32), 'ln_l_w': jnp.ones((DIM,), jnp.float32), 'ln_l_b': jnp.zeros((DIM,), jnp.float32), 'ln_c_w': jnp.ones((DIM,), jnp.float32), 'ln_c_b': jnp.zeros((DIM,), jnp.float32), 'Wq': jax.random.normal(ks[2], (DIM, INNER), jnp.float32) * s, 'Wkv': jax.random.normal(ks[3], (DIM, 2 * INNER), jnp.float32) * s, 'Wo': jax.random.normal(ks[4], (INNER, DIM), jnp.float32) * (1.0 / np.sqrt(INNER)), 'bo': jnp.zeros((DIM,), jnp.float32)}
    _L0_xattn_all = _L0_xattn_setup()
    _L0_xattn_in = {k: v for k, v in _L0_xattn_all.items() if k in ('ln_l_w', 'ln_l_b', 'ln_c_w', 'ln_c_b', 'Wq', 'Wkv', 'Wo', 'bo')}
    del _L0_xattn_all

    def _L0_attn_setup():
        import jax, jax.numpy as jnp
        import numpy as np
        B, S, D, H, DH, FF = (2, 512, 128, 16, 64, 512)

        def _ln(x, g, b):
            m = x.mean(-1, keepdims=True)
            v = ((x - m) ** 2).mean(-1, keepdims=True)
            return (x - m) * jax.lax.rsqrt(v + 1e-05) * g + b

        def _phi(x, proj):
            return jax.nn.elu(x @ proj) + 1.0
        key = jax.random.key(seed)
        ks = jax.random.split(key, 10)
        s = 0.02
        return {'x': jax.random.normal(ks[0], (B, S, D), jnp.float32), 'wq': jax.random.normal(ks[1], (D, H * DH), jnp.float32) * s, 'wk': jax.random.normal(ks[2], (D, H * DH), jnp.float32) * s, 'wv': jax.random.normal(ks[3], (D, H * DH), jnp.float32) * s, 'wo': jax.random.normal(ks[4], (H * DH, D), jnp.float32) * s, 'proj': jax.random.normal(ks[5], (DH, DH), jnp.float32) / np.sqrt(DH).astype(np.float32), 'w1': jax.random.normal(ks[6], (D, FF), jnp.float32) * s, 'b1': jnp.zeros((FF,), jnp.float32), 'w2': jax.random.normal(ks[7], (FF, D), jnp.float32) * s, 'b2': jnp.zeros((D,), jnp.float32), 'g1': jnp.ones((D,), jnp.float32), 'beta1': jnp.zeros((D,), jnp.float32), 'g2': jnp.ones((D,), jnp.float32), 'beta2': jnp.zeros((D,), jnp.float32)}
    _L0_attn_all = _L0_attn_setup()
    _L0_attn_in = {k: v for k, v in _L0_attn_all.items() if k in ('wq', 'wk', 'wv', 'wo', 'proj', 'w1', 'b1', 'w2', 'b2', 'g1', 'beta1', 'g2', 'beta2')}
    del _L0_attn_all

    def _L0_ffn_setup():
        import jax, jax.numpy as jnp
        import numpy as np
        D_MODEL = 128
        D_FF = 512
        NUM_EXPERTS = 8
        key = jax.random.key(seed)
        ks = jax.random.split(key, 8)
        scale_in = 1.0 / np.sqrt(D_MODEL)
        scale_ff = 1.0 / np.sqrt(D_FF)
        x = jax.random.normal(ks[0], (4, 256, D_MODEL), dtype=jnp.float32)
        gate_w = jax.random.uniform(ks[1], (NUM_EXPERTS, D_MODEL), jnp.float32, -scale_in, scale_in)
        gate_b = jax.random.uniform(ks[2], (NUM_EXPERTS,), jnp.float32, -scale_in, scale_in)
        expert_bias = jnp.zeros((NUM_EXPERTS,), dtype=jnp.float32)
        w1 = jax.random.uniform(ks[3], (NUM_EXPERTS, D_MODEL, D_FF), jnp.float32, -scale_in, scale_in)
        b1 = jax.random.uniform(ks[4], (NUM_EXPERTS, D_FF), jnp.float32, -scale_in, scale_in)
        w2 = jax.random.uniform(ks[5], (NUM_EXPERTS, D_FF, D_MODEL), jnp.float32, -scale_ff, scale_ff)
        b2 = jax.random.uniform(ks[6], (NUM_EXPERTS, D_MODEL), jnp.float32, -scale_ff, scale_ff)
        return {'x': x, 'gate_w': gate_w, 'gate_b': gate_b, 'expert_bias': expert_bias, 'w1': w1, 'b1': b1, 'w2': w2, 'b2': b2}
    _L0_ffn_all = _L0_ffn_setup()
    _L0_ffn_in = {k: v for k, v in _L0_ffn_all.items() if k in ('gate_w', 'gate_b', 'expert_bias', 'w1', 'b1', 'w2', 'b2')}
    del _L0_ffn_all
    return {'x': x, 'ctx_1024': ctx_1024, 'L0_xattn_ln_l_w': _L0_xattn_in['ln_l_w'], 'L0_xattn_ln_l_b': _L0_xattn_in['ln_l_b'], 'L0_xattn_ln_c_w': _L0_xattn_in['ln_c_w'], 'L0_xattn_ln_c_b': _L0_xattn_in['ln_c_b'], 'L0_xattn_Wq': _L0_xattn_in['Wq'], 'L0_xattn_Wkv': _L0_xattn_in['Wkv'], 'L0_xattn_Wo': _L0_xattn_in['Wo'], 'L0_xattn_bo': _L0_xattn_in['bo'], 'L0_attn_wq': _L0_attn_in['wq'], 'L0_attn_wk': _L0_attn_in['wk'], 'L0_attn_wv': _L0_attn_in['wv'], 'L0_attn_wo': _L0_attn_in['wo'], 'L0_attn_proj': _L0_attn_in['proj'], 'L0_attn_w1': _L0_attn_in['w1'], 'L0_attn_b1': _L0_attn_in['b1'], 'L0_attn_w2': _L0_attn_in['w2'], 'L0_attn_b2': _L0_attn_in['b2'], 'L0_attn_g1': _L0_attn_in['g1'], 'L0_attn_beta1': _L0_attn_in['beta1'], 'L0_attn_g2': _L0_attn_in['g2'], 'L0_attn_beta2': _L0_attn_in['beta2'], 'L0_ffn_gate_w': _L0_ffn_in['gate_w'], 'L0_ffn_gate_b': _L0_ffn_in['gate_b'], 'L0_ffn_expert_bias': _L0_ffn_in['expert_bias'], 'L0_ffn_w1': _L0_ffn_in['w1'], 'L0_ffn_b1': _L0_ffn_in['b1'], 'L0_ffn_w2': _L0_ffn_in['w2'], 'L0_ffn_b2': _L0_ffn_in['b2']}

def reference(x, ctx_1024, L0_xattn_ln_l_w, L0_xattn_ln_l_b, L0_xattn_ln_c_w, L0_xattn_ln_c_b, L0_xattn_Wq, L0_xattn_Wkv, L0_xattn_Wo, L0_xattn_bo, L0_attn_wq, L0_attn_wk, L0_attn_wv, L0_attn_wo, L0_attn_proj, L0_attn_w1, L0_attn_b1, L0_attn_w2, L0_attn_b2, L0_attn_g1, L0_attn_beta1, L0_attn_g2, L0_attn_beta2, L0_ffn_gate_w, L0_ffn_gate_b, L0_ffn_expert_bias, L0_ffn_w1, L0_ffn_b1, L0_ffn_w2, L0_ffn_b2):
    import jax
    import jax.numpy as jnp

    def _L0_xattn_ref(latents, context, ln_l_w, ln_l_b, ln_c_w, ln_c_b, Wq, Wkv, Wo, bo):
        import jax, jax.numpy as jnp
        import numpy as np
        DIM = 128
        H = 16
        D = 64
        INNER = H * D
        EPS = 1e-05

        def layernorm(x, w, b):
            mu = jnp.mean(x, axis=-1, keepdims=True)
            var = jnp.var(x, axis=-1, keepdims=True)
            return (x - mu) * jax.lax.rsqrt(var + EPS) * w + b
        b, n, _ = latents.shape
        s = context.shape[1]
        lat = layernorm(latents, ln_l_w, ln_l_b)
        ctx = layernorm(context, ln_c_w, ln_c_b)
        q = (lat @ Wq).reshape(b, n, H, D).transpose(0, 2, 1, 3)
        kv = ctx @ Wkv
        k, v = jnp.split(kv, 2, axis=-1)
        k = k.reshape(b, s, H, D).transpose(0, 2, 1, 3)
        v = v.reshape(b, s, H, D).transpose(0, 2, 1, 3)
        scale = D ** (-0.5)
        attn = jnp.einsum('bhnd,bhsd->bhns', q, k) * scale
        attn = jnp.clip(attn, -11.0, 11.0)
        attn = jax.nn.softmax(attn, axis=-1)
        out = jnp.einsum('bhns,bhsd->bhnd', attn, v)
        out = out.transpose(0, 2, 1, 3).reshape(b, n, INNER)
        return out @ Wo + bo

    def _L0_attn_ref(x, wq, wk, wv, wo, proj, w1, b1, w2, b2, g1, beta1, g2, beta2):
        import jax, jax.numpy as jnp
        import numpy as np
        B, S, D, H, DH, FF = (2, 512, 128, 16, 64, 512)

        def _ln(x, g, b):
            m = x.mean(-1, keepdims=True)
            v = ((x - m) ** 2).mean(-1, keepdims=True)
            return (x - m) * jax.lax.rsqrt(v + 1e-05) * g + b

        def _phi(x, proj):
            return jax.nn.elu(x @ proj) + 1.0
        b, s, d = x.shape
        h = _ln(x, g1, beta1)
        q = _phi((h @ wq).reshape(b, s, H, DH), proj)
        k = _phi((h @ wk).reshape(b, s, H, DH), proj)
        v = (h @ wv).reshape(b, s, H, DH)
        qs = jnp.moveaxis(q, 1, 0)
        ks_ = jnp.moveaxis(k, 1, 0)
        vs = jnp.moveaxis(v, 1, 0)

        def step(carry, qkv_t):
            kv, ksum = carry
            q_t, k_t, v_t = qkv_t
            kv = kv + k_t[..., :, None] * v_t[..., None, :]
            ksum = ksum + k_t
            num = jnp.einsum('bhd,bhde->bhe', q_t, kv)
            den = jnp.einsum('bhd,bhd->bh', q_t, ksum) + 1e-06
            return ((kv, ksum), num / den[..., None])
        kv0 = jnp.zeros((b, H, DH, DH), x.dtype)
        ks0 = jnp.zeros((b, H, DH), x.dtype)
        _, outs = jax.lax.scan(step, (kv0, ks0), (qs, ks_, vs))
        attn = jnp.moveaxis(outs, 0, 1).reshape(b, s, H * DH) @ wo
        x = x + attn
        h2 = _ln(x, g2, beta2)
        x = x + (jax.nn.gelu(h2 @ w1 + b1, approximate=False) @ w2 + b2)
        return x

    def _L0_ffn_ref(x, gate_w, gate_b, expert_bias, w1, b1, w2, b2):
        import jax, jax.numpy as jnp
        import numpy as np
        D_MODEL = 128
        D_FF = 512
        NUM_EXPERTS = 8
        gate_logits = jnp.einsum('bsd,ed->bse', x, gate_w) + gate_b + expert_bias
        top_idx = jnp.argmax(gate_logits, axis=-1)
        out = jnp.zeros_like(x)
        for e in range(NUM_EXPERTS):
            mask = (top_idx == e)[..., None].astype(x.dtype)
            h = jax.nn.relu(jnp.einsum('bsd,df->bsf', x, w1[e]) + b1[e])
            y = jnp.einsum('bsf,fd->bsd', h, w2[e]) + b2[e]
            out = out + mask * y
        return out
    x = x + _L0_xattn_ref(_layernorm(x, axis=-1), ctx_1024, L0_xattn_ln_l_w, L0_xattn_ln_l_b, L0_xattn_ln_c_w, L0_xattn_ln_c_b, L0_xattn_Wq, L0_xattn_Wkv, L0_xattn_Wo, L0_xattn_bo)
    x = x + _L0_attn_ref(_layernorm(x, axis=-1), L0_attn_wq, L0_attn_wk, L0_attn_wv, L0_attn_wo, L0_attn_proj, L0_attn_w1, L0_attn_b1, L0_attn_w2, L0_attn_b2, L0_attn_g1, L0_attn_beta1, L0_attn_g2, L0_attn_beta2)
    x = x + _L0_ffn_ref(_layernorm(x, axis=-1), L0_ffn_gate_w, L0_ffn_gate_b, L0_ffn_expert_bias, L0_ffn_w1, L0_ffn_b1, L0_ffn_w2, L0_ffn_b2)
    return x

_drawn_inputs = setup_inputs


def setup_inputs(seed=0):
    import zlib

    import numpy as np

    out = dict(_drawn_inputs(seed))
    spreads = {'L0_xattn_ln_l_w': (1.0, 0.2),
     'L0_xattn_ln_l_b': (0.0, 0.294),
     'L0_xattn_ln_c_w': (1.0, 0.2),
     'L0_xattn_ln_c_b': (0.0, 0.1),
     'L0_xattn_bo': (0.0, 0.1),
     'L0_attn_b1': (0.0, 0.366),
     'L0_attn_b2': (0.0, 0.1),
     'L0_attn_g1': (1.0, 0.6),
     'L0_attn_beta1': (0.0, 0.8),
     'L0_attn_g2': (1.0, 0.6),
     'L0_attn_beta2': (0.0, 0.8),
     'L0_ffn_expert_bias': (0.0, 0.1)}
    factors = {'L0_attn_wq': 8.0,
     'L0_attn_wk': 8.0,
     'L0_attn_proj': 8.0,
     'L0_ffn_b1': 5.879,
     'L0_ffn_b2': 4.738}
    for name, (base, spread) in spreads.items():
        noise = np.random.default_rng([zlib.crc32(name.encode()), seed]).standard_normal(out[name].shape)
        drawn = base * np.exp(spread * noise) if base else spread * noise
        out[name] = jnp.asarray(drawn.astype(out[name].dtype))
    for name, factor in factors.items():
        out[name] = (out[name] * factor).astype(out[name].dtype)
    return out
```

```python
import concourse.bass as bass
from concourse import mybir
from contextlib import ExitStack

NB, NL, D = 32, 64, 128
NC = 128
H, DH = 16, 64
INNER = H * DH
FF = 512
NE = 8
P = 128
NG = 8
BG = NB // NG
JG = BG // 2
TG = BG * NL
NT = NB * NL // P
RING = 4
NS = -(-(NT + NE - 1) // RING) * RING
REC = 2 * D + 1
NOBODY = 2 * NB * NL - 1
EPS = 1e-5
SCALE = DH ** -0.5
CLIP = 11.0


class Banks:

    def __init__(self, first, number, chunks, before):
        self.place = {c: (first + n % number, n // number) for n, c in enumerate(chunks)}
        self.uses = {first + m: len(range(m, len(chunks), number)) for m in range(number)}
        self.before = dict.fromkeys(self.uses, before) if isinstance(before, int) else before

    def bank(self, chunk):
        return self.place[chunk][0]

    def count(self, chunk, g):
        bank, use = self.place[chunk]
        return g * self.uses[bank] + (self.before[bank] + use)

    def after(self, groups):
        return {bank: self.before[bank] + groups * uses for bank, uses in self.uses.items()}

    def needs(self, chunk, reads, g):
        last = {}
        for bank, uses in [self.place[chunk]] + [(self.place[c][0], self.place[c][1] + 1) for c in reads]:
            last[bank] = max(uses, last.get(bank, 0))
        return [(bank, g * self.uses[bank] + (self.before[bank] + uses)) for bank, uses in last.items()]


def perceiver_layer(nc, x, ctx, wts, out, slots):
    F32 = mybir.dt.float32
    U32 = mybir.dt.uint32
    I32 = mybir.dt.int32
    AX = mybir.AxisListType
    ALU = mybir.AluOpType
    ACT = mybir.ActivationFunctionType

    x_v = x.rearrange("b n d -> (b n) d").rearrange("(g j p) d -> g p j d", j=JG, p=P)
    out_rows = out.rearrange("b n d -> (b n) d")
    slots_v = slots.rearrange("(n p) c -> n p c", p=P)
    ctx_v = ctx.rearrange("(g b) s d -> g s b d", b=BG)

    X = Banks(0, 4, ["lat", "ctx"] + [("t", k) for k in range(8)]
              + [c for j in range(JG) for c in
                 [(n, 2 * j + b, c) for b in range(2) for n in "SV" for c in range(2)]
                 + [("PV", j, q) for q in range(4)] + [("T", j, c) for c in range(2)] + [("Wo", j)]], 2)
    L = Banks(4, 3, ["h"] + [("qk", k) for k in range(8)]
              + [c for j in range(JG) for c in
                 [("v", j, c) for c in range(2)] + [("A", j, p) for p in range(2)]
                 + [("AV", j, q) for q in range(4)] + [("T", j, c) for c in range(2)] + [("wo", j)]], 2)
    F = Banks(7, 1, ["h", ("w1", 0), ("w1", 1), "w2", "zr", "gate"], 3)
    R = Banks(7, 1, ["rank"], F.after(NG))
    E = Banks(0, 8, [(n, r) for r in range(RING) for n in ("z", "hA", "hB", "y")],
              {**X.after(NG), **L.after(NG), **R.after(1)})

    es = ExitStack()
    with es:
        def sb(name, shape, dt=F32):
            return es.enter_context(nc.sbuf_tensor(name, shape, dt))

        def sem(name):
            return es.enter_context(nc.semaphore(name))

        ident = sb("ident", [P, P])
        causal = sb("causal", [P, NL])
        minus_half = sb("minus_half", [P, 8])
        absorbed = sb("absorbed", [P, H, P])
        wv_x = sb("wv_x", [P, INNER])
        wo_x = sb("wo_x", [P, 8, P])
        wq_phi = sb("wq_phi", [P, INNER])
        wk_phi = sb("wk_phi", [P, INNER])
        wv_l = sb("wv_l", [P, INNER])
        wo_l = sb("wo_l", [P, 8, P])
        w1 = sb("w1", [P, FF])
        w2 = sb("w2", [P, 4, P])
        proj2 = sb("proj2", [P, DH])
        cols = sb("cols", [P, 12])
        bo_row = sb("bo_row", [P, D])
        b2_row = sb("b2_row", [P, D])
        state = sb("state", [P, NB // 2, D])
        ctx_in = sb("ctx_in", [P, BG, D])
        z_in = sb("z_in", [P, JG + BG, D])
        lat_t = sb("lat_t", [P, TG])
        ctx_t = sb("ctx_t", [P, BG * NC])
        t_t = sb("t_t", [P, H, TG])
        clipped = sb("clipped", [P, 2, 512])
        probs = sb("probs", [P, 2, H * NL])
        v_x = sb("v_x", [P, 2, H, DH + 1])
        o_x = sb("o_x", [P, INNER])
        ot_x = sb("ot_x", [P, INNER])
        x_plus_bo = sb("x_plus_bo", [P, JG, D])
        z_res = sb("z_res", [P, JG, D])
        h_z = sb("h_z", [P, JG, D])
        h_t = sb("h_t", [P, TG])
        qk_t = sb("qk_t", [P, 16, TG])
        q_t, k_t = qk_t[:, 0:8, :], qk_t[:, 8:16, :]
        neg_relu = sb("neg_relu", [P, 2, 512])
        phi_exp = sb("phi_exp", [P, 2, 512])
        v_l = sb("v_l", [P, H, DH + 1])
        a_t = sb("a_t", [P, 2, 8, NL])
        o_l = sb("o_l", [P, INNER])
        ot_l = sb("ot_l", [P, INNER])
        zf = sb("zf", [P, JG, D])
        zf_b2 = sb("zf_b2", [P, JG, D])
        f_z = sb("f_z", [P, JG, D])
        f_t = sb("f_t", [P, TG])
        g_t = sb("g_t", [P, 4, TG])
        f_sum = sb("f_sum", [P, JG, D])
        records = sb("records", [P, NT, REC])
        z_r = sb("z_r", [P, JG, D])
        zr_t = sb("zr_t", [P, TG])
        gate_in = sb("gate_in", [NE, D])
        b1_in = sb("b1_in", [NE * 4, P])
        gate_b1_t = sb("gate_b1_t", [P, NE + NE * 4])
        gate_b_row = sb("gate_b_row", [P, NE])
        expert_bias_row = sb("expert_bias_row", [P, NE])
        logits = sb("logits", [P, NT, NE])
        expert_m8 = sb("expert_m8", [P, NE])
        thresholds = sb("thresholds", [P, NT])
        tile_no = sb("tile_no", [P, NS])
        earlier_expert = sb("earlier_expert", [P, NE, NE])
        earlier_row = sb("earlier_row", [P, P])
        ones = sb("ones", [P, P])
        iota_e = sb("iota_e", [P, NE])
        tile_ends = sb("tile_ends", [1, NS, NE])
        work = [sb(f"work{n}", [P, NT * NE]) for n in range(4)]
        chosen = sb("chosen", [P, NT, NE])
        best = sb("best", [P, 2, NT])
        tiles_of = sb("tiles_of", [P, 3, NE])
        per_tile = sb("per_tile", [P, NS])
        expert_of = sb("expert_of", [P, NS], I32)
        slot_of = sb("slot_of", [P, NT], U32)
        empty_record = sb("empty_record", [P, REC])
        st_r = sb("st_r", [P, JG, 6])
        mv_r = sb("mv_r", [P, JG, 2])
        var_r = sb("var_r", [P, JG])
        rstd_r = sb("rstd_r", [P, JG])
        e_w1 = qk_t[:].rearrange("p a b -> p (a b)").rearrange("p (e f) -> p e f", e=NE)
        e_w2 = t_t[:].rearrange("p a b -> p (a b)").rearrange("p (k d) -> p k d", d=D)
        e_b2 = sb("e_b2", [P, NE * D])
        slot_in = sb("slot_in", [P, RING, REC])
        slot_t = sb("slot_t", [P, 2, P])
        w1_now = sb("w1_now", [P, 2, FF])
        hid_t = sb("hid_t", [P, 2, 4, P])
        x2_b2 = sb("x2_b2", [P, 2, D])
        slot_out = sb("slot_out", [P, RING, D])
        st_in = sb("st_in", [P, JG + BG, 6])
        mv_in = sb("mv_in", [P, JG + BG, 2])
        var_in = sb("var_in", [P, JG + BG])
        rstd_in = sb("rstd_in", [P, JG + BG])
        st_x1 = sb("st_x1", [P, JG, 6])
        mv_x1 = sb("mv_x1", [P, JG, 2])
        var_x1 = sb("var_x1", [P, 2, JG])
        rstd_x1 = sb("rstd_x1", [P, 2, JG])
        st_z = sb("st_z", [P, JG, 6])
        mv_z = sb("mv_z", [P, JG, 2])
        var_z = sb("var_z", [P, JG])
        rstd_z = sb("rstd_z", [P, JG])
        den = sb("den", [P, 2, 4])
        rden = sb("rden", [P, 2, 4])

        ps = [es.enter_context(nc.psum_tensor(f"bank{n}", [P, 512], F32)) for n in range(8)]

        raw = {"Wq": q_t[:, 0:4, :], "Wk": q_t[:, 4:8, :], "wq": k_t[:, 0:4, :], "wk": k_t[:, 4:8, :]}
        raw = {n: v.rearrange("p a b -> p (a b)") for n, v in raw.items()}
        raw_t = {"Wq": t_t[:, 0:4, :], "Wk": t_t[:, 4:8, :], "wq": t_t[:, 8:12, :], "wk": t_t[:, 12:16, :]}
        raw_t = {n: v.rearrange("p a b -> p (a b)").rearrange("p (c m) -> p c m", m=P)
                 for n, v in raw_t.items()}

        bank_filled = [sem(f"bank_filled{n}") for n in range(8)]
        bank_drained = [sem(f"bank_drained{n}") for n in range(8)]
        ident_zeroed = sem("ident_zeroed")
        causal_half = sem("causal_half")
        consts_ready = sem("consts_ready")
        rows_loaded = sem("rows_loaded")
        raw_loaded = sem("raw_loaded")
        weights_loaded = sem("weights_loaded")
        cols_loaded = sem("cols_loaded")
        x_loaded = sem("x_loaded")
        ctx_loaded = sem("ctx_loaded")
        pe_waits_passed, dve_waits_passed = sem("pe_waits_passed"), sem("dve_waits_passed")
        pool_waits_passed = sem("pool_waits_passed")
        in_step, x_step, l_step = sem("in_step"), sem("x_step"), sem("l_step")
        var_in_ready, rstd_in_ready = sem("var_in_ready"), sem("rstd_in_ready")
        var_x1_ready, rstd_x1_ready = sem("var_x1_ready"), sem("rstd_x1_ready")
        var_z_ready, rstd_z_ready = sem("var_z_ready"), sem("rstd_z_ready")
        z_in_ready = sem("z_in_ready")
        h_z_ready = sem("h_z_ready")
        f_z_ready = sem("f_z_ready")
        probs_ready = sem("probs_ready")
        relu_ready, phi_exp_ready = sem("relu_ready"), sem("phi_exp_ready")
        bo_added = sem("bo_added")
        b2_added = sem("b2_added")
        var_r_ready, rstd_r_ready = sem("var_r_ready"), sem("rstd_r_ready")
        z_r_ready = sem("z_r_ready")
        f_step, route_step = sem("f_step"), sem("route_step")
        empty_ready = sem("empty_ready")
        routing_consts = sem("routing_consts")
        slots_emptied = sem("slots_emptied")
        e_w1_loaded, e_w2_loaded = sem("e_w1_loaded"), sem("e_w2_loaded")
        chosen_ready = sem("chosen_ready")
        experts_known, slots_known = sem("experts_known"), sem("slots_known")
        slots_written = sem("slots_written")
        slot_loaded = [sem(f"slot_loaded{r}") for r in range(RING)]
        w1_now_ready = sem("w1_now_ready")
        b2_ready = sem("b2_ready")
        tokens_written = [sem(f"tokens_written{r}") for r in range(RING)]

        RAW = ("Wq", "Wk", "wq", "wk")
        NRAW, NWTS, NCOLS, NROWS = 8, 6, 12, 5

        block = es.enter_context(nc.Block())

        def steps(engine, step):
            step(0, None, None, 1)
            step(1, 0, None, 2)
            with engine.Fori(2, NG - 1) as g:
                step(g, g - 1, g - 2, g + 1)
            step(NG - 1, NG - 2, NG - 3, None)
            step(None, NG - 1, NG - 2, None)
            step(None, None, NG - 1, None)

        def tile_steps(engine, tiles):
            tiles(0, True, False)
            with engine.Fori(1, NS // RING - 1) as i:
                tiles(i, False, False)
            tiles(NS // RING - 1, False, True)

        @block.sync
        def _(sp):
            sp.dma_start(state[:, 0:JG, :], x_v[0]).then_inc(x_loaded, 16)
            sp.dma_start(ctx_in[:], ctx_v[0]).then_inc(ctx_loaded, 16)
            sp.dma_start(raw["Wq"], wts["Wq"]).then_inc(raw_loaded, 16)
            sp.dma_start(raw["Wk"], wts["Wkv"][:, 0:INNER]).then_inc(raw_loaded, 16)
            sp.dma_start(raw["wq"], wts["wq"]).then_inc(raw_loaded, 16)
            sp.dma_start(raw["wk"], wts["wk"]).then_inc(raw_loaded, 16)
            for half in range(2):
                sp.dma_start(proj2[half * DH:(half + 1) * DH, :], wts["proj"]).then_inc(raw_loaded, 16)
            sp.dma_start(gate_in[:], wts["gate_w"]).then_inc(raw_loaded, 16)
            sp.dma_start(b1_in[:], wts["e_b1"].rearrange("e f -> (e f)").rearrange("(k p) -> k p", p=P))\
              .then_inc(raw_loaded, 16)
            sp.dma_start(wv_x[:], wts["Wkv"][:, INNER:2 * INNER]).then_inc(weights_loaded, 16)
            sp.dma_start(wo_x[:], wts["Wo"].rearrange("(c p) n -> p c n", p=P)).then_inc(weights_loaded, 16)
            sp.dma_start(wv_l[:], wts["wv"]).then_inc(weights_loaded, 16)
            sp.dma_start(wo_l[:], wts["wo"].rearrange("(c p) n -> p c n", p=P)).then_inc(weights_loaded, 16)
            sp.dma_start(w1[:], wts["w1"]).then_inc(weights_loaded, 16)
            sp.dma_start(w2[:], wts["w2"].rearrange("(c p) n -> p c n", p=P)).then_inc(weights_loaded, 16)
            sp.dma_start(state[:, JG:, :].rearrange("p (g j) d -> p g j d", j=JG),
                         x_v[1:NG].rearrange("g p j d -> p g j d")).then_inc(x_loaded, 16)
            with sp.Fori(1, NG) as g:
                sp.wait_ge(z_in_ready, g)
                sp.dma_start(ctx_in[:], ctx_v[g]).then_inc(ctx_loaded, 16)
            sp.wait_ge(empty_ready, 3)
            sp.dma_start(slots_v.rearrange("n p c -> p n c"),
                         empty_record[:].unsqueeze(1).to_broadcast([P, NS, REC])).then_inc(slots_emptied, 16)
            sp.wait_ge(bank_filled[X.bank(("S", BG - 1, 1))], X.count(("S", BG - 1, 1), NG - 1) + 1)
            sp.dma_start(e_w2, wts["e_w2"].rearrange("e f d -> (e f) d").rearrange("(k p) d -> p k d", p=P))\
              .then_inc(e_w2_loaded, 16)
            sp.wait_ge(bank_filled[L.bank(("A", JG - 1, 1))], L.count(("A", JG - 1, 1), NG - 1) + 1)
            sp.dma_start(e_w1, wts["e_w1"].rearrange("e d f -> d e f")).then_inc(e_w1_loaded, 16)
            sp.wait_ge(slots_written, 16 * NT)
            for r in range(RING):
                sp.dma_start(slot_in[:, r, :], slots_v[r]).then_inc(slot_loaded[r], 16)
            with sp.Fori(1, NS // RING) as i:
                for r in range(RING):
                    sp.wait_ge(tokens_written[r], 16 * i)
                    sp.dma_start(slot_in[:, r, :], slots_v[RING * i + r]).then_inc(slot_loaded[r], 16)
            for r in range(RING):
                sp.wait_ge(tokens_written[r], 16 * (NS // RING))

        @block.tensor
        def _(pe):
            mm = nc.tensor.matmul

            pe.wait_ge(consts_ready, 2)
            pe.wait_ge(raw_loaded, 16 * NRAW)
            for n in range(8):
                for m in range(4):
                    c = 4 * (n % 2) + m
                    last = nc.tensor.transpose(ps[n][:, m * P:(m + 1) * P],
                                               raw[RAW[n // 2]][:, c * P:(c + 1) * P], ident[:])
                last.then_inc(bank_filled[n], 1)
            for n in range(8):
                pe.wait_ge(bank_drained[n], 1)
            for n in range(8):
                par = slice((n % 2) * DH, (n % 2 + 1) * DH)
                if n < 4:
                    for m in range(4):
                        c = 4 * (n // 2) + m
                        last = mm(ps[n][:, m * P:(m + 1) * P], raw_t["Wq"][par, c, :],
                                  raw_t["Wk"][par, c, :], start=True, stop=True)
                else:
                    for c in range(8):
                        last = mm(ps[n][:, c * DH:(c + 1) * DH], raw_t[RAW[n // 2]][par, c, :],
                                  proj2[par, :], start=True, stop=True)
                last.then_inc(bank_filled[n], 1)
            pe.wait_ge(bank_drained[7], 2)
            nc.tensor.transpose(ps[7][:, 0:NE], gate_in[:], ident[0:NE, 0:NE])
            nc.tensor.transpose(ps[7][:, NE:NE + 4 * NE], b1_in[:], ident[0:4 * NE, 0:4 * NE])\
              .then_inc(bank_filled[7], 1)
            for n in range(8):
                pe.wait_ge(bank_drained[n], 3 if n == 7 else 2)
            pe.wait_ge(weights_loaded, 16 * NWTS)

            def waits_alone():
                pe.sem_inc(pe_waits_passed, 1)

            def chunk(stage, name, g, reads=()):
                for bank, count in stage.needs(name, reads, g):
                    pe.wait_ge(bank_drained[bank], count)
                bank = stage.bank(name)
                return ps[bank], bank_filled[bank]

            def transposes(stage, name, g, z, n0, n1):
                bank, filled = chunk(stage, name, g)
                for n in range(n0, n1):
                    last = nc.tensor.transpose(bank[:, (n - n0) * P:(n - n0 + 1) * P], z[:, n, :], ident[:])
                last.then_inc(filled, 1)

            def x_inputs(g):
                pe.wait_ge(z_in_ready, g + 1)
                transposes(X, "lat", g, z_in, 0, JG)
                transposes(X, "ctx", g, z_in, JG, JG + BG)

            def x_t(g, k):
                bank, filled = chunk(X, ("t", k), g, ["lat"] if k == 0 else [])
                for m in range(2):
                    last = mm(bank[:, m * TG:(m + 1) * TG], absorbed[:, 2 * k + m, :], lat_t[:],
                              start=True, stop=True)
                last.then_inc(filled, 1)

            def x_scores(g, b):
                for c in range(2):
                    reads = ["ctx"] + [("t", k) for k in range(8)] if (b, c) == (0, 0) else []
                    bank, filled = chunk(X, ("S", b, c), g, reads)
                    mm(bank[:], ctx_t[:, b * NC:(b + 1) * NC], t_t[:, 8 * c:8 * c + 8, b * NL:(b + 1) * NL],
                       start=True, stop=True).then_inc(filled, 1)

            def x_values(g, b):
                for c in range(2):
                    bank, filled = chunk(X, ("V", b, c), g)
                    mm(bank[:], ctx_t[:, b * NC:(b + 1) * NC], wv_x[:, c * 512:(c + 1) * 512],
                       start=True, stop=True).then_inc(filled, 1)

            def x_pv(g, j):
                pe.wait_ge(probs_ready, g * (2 * BG) + (4 * j + 4))
                for q in range(4):
                    reads = [("V", 2 * j + b, c) for b in range(2) for c in range(2)] if q == 0 else []
                    bank, filled = chunk(X, ("PV", j, q), g, reads)
                    for m in range(4):
                        h = 4 * q + m
                        for b in range(2):
                            last = mm(bank[b * NL:(b + 1) * NL, m * (DH + 1):(m + 1) * (DH + 1)],
                                      probs[:, b, h * NL:(h + 1) * NL], v_x[:, b, h, :],
                                      start=True, stop=True)
                    last.then_inc(filled, 1)

            def turn(stage, j, g, o, heads):
                for c in range(2):
                    bank, filled = chunk(stage, ("T", j, c), g, [(heads, j, 2 * c), (heads, j, 2 * c + 1)])
                    for m in range(4):
                        last = nc.tensor.transpose(bank[:, m * P:(m + 1) * P],
                                                   o[:, (4 * c + m) * P:(4 * c + m + 1) * P], ident[:])
                    last.then_inc(filled, 1)

            def out_projection(stage, j, g, ot, wo, name):
                bank, filled = chunk(stage, (name, j), g, [("T", j, 0), ("T", j, 1)])
                for c in range(8):
                    last = mm(bank[:, 0:D], ot[:, c * P:(c + 1) * P], wo[:, c, :],
                              start=(c == 0), stop=(c == 7))
                last.then_inc(filled, 1)

            def l_inputs(g):
                pe.wait_ge(h_z_ready, g + 1)
                transposes(L, "h", g, h_z, 0, JG)

            def l_qk(g, k):
                bank, filled = chunk(L, ("qk", k), g, ["h"] if k == 0 else [])
                w = wq_phi if k < 4 else wk_phi
                for m in range(2):
                    c = 2 * (k % 4) + m
                    last = mm(bank[:, m * TG:(m + 1) * TG], w[:, c * P:(c + 1) * P], h_t[:],
                              start=True, stop=True)
                last.then_inc(filled, 1)

            def l_values(g, j):
                for c in range(2):
                    bank, filled = chunk(L, ("v", j, c), g)
                    mm(bank[:], h_t[:, j * P:(j + 1) * P], wv_l[:, c * 512:(c + 1) * 512],
                       start=True, stop=True).then_inc(filled, 1)

            def l_scores(g, j):
                for par in range(2):
                    rows = slice(par * DH, (par + 1) * DH)
                    reads = [("qk", k) for k in range(8)] if (j, par) == (0, 0) else []
                    bank, filled = chunk(L, ("A", j, par), g, reads)
                    waits_alone()
                    for c in range(8):
                        for b in range(2):
                            tok = slice(j * P + b * NL, j * P + (b + 1) * NL)
                            last = mm(bank[b * NL:(b + 1) * NL, c * NL:(c + 1) * NL],
                                      k_t[rows, c, tok], q_t[rows, c, tok], start=True, stop=True)
                    last.then_inc(filled, 1)

            def l_av(g, j):
                reads = [("A", j, 0), ("A", j, 1), ("v", j, 0), ("v", j, 1)]
                for q0 in (0, 2):
                    banks = [chunk(L, ("AV", j, q0 + n), g, reads if q0 + n == 0 else []) for n in range(2)]
                    waits_alone()
                    for b in range(2):
                        rows = slice(b * NL, (b + 1) * NL)
                        for n, (bank, filled) in enumerate(banks):
                            for m in range(4):
                                h = 4 * (q0 + n) + m
                                last = mm(bank[rows, m * (DH + 1):(m + 1) * (DH + 1)],
                                          a_t[rows, h % 2, h // 2, :], v_l[rows, h, :],
                                          start=True, stop=True)
                            if b == 1:
                                last.then_inc(filled, 1)

            def f_inputs(g):
                pe.wait_ge(f_z_ready, g + 1)
                transposes(F, "h", g, f_z, 0, JG)

            def f_up(g, n):
                bank, filled = chunk(F, ("w1", n), g, ["h"] if n == 0 else [])
                for m in range(2):
                    c = 2 * n + m
                    last = mm(bank[:, m * TG:(m + 1) * TG], w1[:, c * P:(c + 1) * P], f_t[:],
                              start=True, stop=True)
                last.then_inc(filled, 1)

            def f_down(g):
                bank, filled = chunk(F, "w2", g, [("w1", 1)])
                for j in range(JG):
                    for c in range(4):
                        last = mm(bank[:, j * D:(j + 1) * D], g_t[:, c, j * P:(j + 1) * P], w2[:, c, :],
                                  start=(c == 0), stop=(c == 3))
                last.then_inc(filled, 1)

            def r_inputs(g):
                pe.wait_ge(z_r_ready, g + 1)
                transposes(F, "zr", g, z_r, 0, JG)

            def r_gate(g):
                bank, filled = chunk(F, "gate", g, ["zr"])
                for j in range(JG):
                    last = mm(bank[:, j * NE:(j + 1) * NE], zr_t[:, j * P:(j + 1) * P], gate_b1_t[:, 0:NE],
                              start=True, stop=True)
                last.then_inc(filled, 1)

            def step(gx, gl, gf, gi):
                if gx is not None:
                    x_inputs(gx)
                    x_t(gx, 0)
                    x_t(gx, 1)
                if gl is not None:
                    l_inputs(gl)
                if gf is not None:
                    f_inputs(gf)
                for k in range(8):
                    if gx is not None and k + 2 < 8:
                        x_t(gx, k + 2)
                    if gf is not None and k == 4:
                        f_up(gf, 0)
                    if gl is not None:
                        l_qk(gl, k)
                    if gf is not None and k == 4:
                        f_up(gf, 1)
                if gf is not None:
                    f_down(gf)
                for j in range(JG):
                    if gx is not None:
                        for b in (2 * j, 2 * j + 1):
                            x_scores(gx, b)
                            x_values(gx, b)
                    if gl is not None:
                        l_values(gl, j)
                        l_scores(gl, j)
                        l_av(gl, j)
                    if gx is not None:
                        x_pv(gx, j)
                    if gl is not None:
                        turn(L, j, gl, o_l, "AV")
                    if gx is not None:
                        turn(X, j, gx, o_x, "PV")
                    if gl is not None:
                        out_projection(L, j, gl, ot_l, wo_l, "wo")
                    if gx is not None:
                        out_projection(X, j, gx, ot_x, wo_x, "Wo")
                    if gf is not None and j == 0:
                        r_inputs(gf)
                        r_gate(gf)

            steps(pe, step)

            pe.wait_ge(chosen_ready, 1)
            bank, filled = chunk(R, "rank", 0)
            flat = chosen[:].rearrange("p t e -> p (t e)")
            mm(bank[:, 0:NT * NE], earlier_row[:], flat, start=True, stop=True)
            mm(bank[:, NT * NE:2 * NT * NE], ones[:], flat, start=True, stop=True).then_inc(filled, 1)

            def e_z(i, r):
                pe.wait_ge(slot_loaded[r], 16 * i + 16)
                bank, filled = chunk(E, ("z", r), i)
                nc.tensor.transpose(bank[:, 0:P], slot_in[:, r, 0:D], ident[:]).then_inc(filled, 1)

            def e_up(i, r):
                pe.wait_ge(w1_now_ready, RING * i + (r + 1))
                for n, name in enumerate(("hA", "hB")):
                    bank, filled = chunk(E, (name, r), i, [("z", r)])
                    for m in range(2):
                        c = 2 * n + m
                        last = mm(bank[:, m * P:(m + 1) * P], w1_now[:, r % 2, c * P:(c + 1) * P],
                                  slot_t[:, r % 2, :], start=True, stop=True)
                    last.then_inc(filled, 1)

            def e_down(i, r, expert):
                bank, filled = chunk(E, ("y", r), i, [("hA", r), ("hB", r)])
                for c in range(4):
                    last = mm(bank[:, 0:D], hid_t[:, r % 2, c, :], e_w2[:, expert * 4 + c, :],
                              start=(c == 0), stop=(c == 3))
                last.then_inc(filled, 1)

            def tiles(i, first, last):
                def expert(n):
                    return pe.value_load(expert_of[0:1, bass.ds(n, 1)], min_val=0, max_val=NE - 1)
                if first:
                    e_z(i, 0)
                for r in range(RING):
                    if r + 1 < RING:
                        e_z(i, r + 1)
                    elif not last:
                        e_z(i + 1, 0)
                    e_up(i, r)
                    if r > 0:
                        e_down(i, r - 1, expert(RING * i + (r - 1)))
                    elif not first:
                        e_down(i - 1, RING - 1, expert(RING * i - 1))
                if last:
                    e_down(i, RING - 1, expert(RING * i + RING - 1))

            pe.wait_ge(experts_known, 1)
            pe.wait_ge(e_w2_loaded, 16)
            tile_steps(pe, tiles)

        @block.scalar
        def _(act):
            for n, name in enumerate(["ln_l_w", "ln_l_b", "ln_c_w", "ln_c_b", "g1", "beta1", "g2", "beta2"]):
                act.dma_start(cols[:, n:n + 1], wts[name].rearrange("(p a) -> p a", a=1)).then_inc(cols_loaded, 16)
            for c in range(4):
                act.dma_start(cols[:, 8 + c:9 + c], wts["b1"][c * P:(c + 1) * P].rearrange("(p a) -> p a", a=1))\
                   .then_inc(cols_loaded, 16)
            for n in range(0, 8, 2):
                act.wait_ge(bank_filled[n], 1)
                nc.scalar.activation(raw_t[RAW[n // 2]][:, 0:4, :], ps[n][:].rearrange("p (c m) -> p c m", m=P),
                                     ACT.Copy).then_inc(bank_drained[n], 1)
            for n in range(0, 8, 2):
                act.wait_ge(bank_filled[n], 2)
                if n < 4:
                    dst = absorbed[:, 8 * (n // 2):8 * (n // 2) + 8:2, :]
                    src = ps[n][:].rearrange("p (c m) -> p c m", m=P)
                else:
                    dst = (wq_phi if n == 4 else wk_phi)[:].rearrange("p (c h e) -> p c h e", h=2, e=DH)[:, :, 0, :]
                    src = ps[n][:].rearrange("p (c e) -> p c e", e=DH)
                nc.scalar.activation(dst, src, ACT.Copy).then_inc(bank_drained[n], 1)
            act.wait_ge(cols_loaded, 16 * NCOLS)

            def filled(stage, name, g):
                bank = stage.bank(name)
                act.wait_ge(bank_filled[bank], stage.count(name, g) + 1)
                return ps[bank], bank_drained[bank]

            def taken(stage, name, g):
                act.wait_ge(bank_drained[stage.bank(name)], stage.count(name, g) + 1)

            def copy_out(stage, name, g, dst, src=lambda bank: bank[:]):
                bank, drained = filled(stage, name, g)
                nc.scalar.activation(dst, src(bank), ACT.Copy).then_inc(drained, 1)

            def x_t(g, k):
                copy_out(X, ("t", k), g, t_t[:, 2 * k:2 * k + 2, :],
                         lambda bank: bank[:].rearrange("p (m t) -> p m t", m=2))

            def values(stage, name, g, dst):
                copy_out(stage, name, g, dst, lambda bank: bank[:].rearrange("p (h e) -> p h e", e=DH))

            def x_exp(g, b, c):
                n = 2 * b + c
                taken(X, ("S", b, c), g)
                nc.scalar.activation(probs[:, b % 2, c * 512:(c + 1) * 512], clipped[:, n % 2, :], ACT.Exp,
                                     scale=SCALE).then_inc(probs_ready, 1)

            def l_relu(g, k):
                bank, _ = filled(L, ("qk", k), g)
                nc.scalar.activation(neg_relu[:, k % 2, :], bank[:], ACT.Relu, scale=-1.0).then_inc(relu_ready, 1)

            def l_exp(g, k):
                act.wait_ge(relu_ready, g * 8 + (k + 1))
                if k >= 2:
                    taken(L, ("qk", k - 2), g)
                nc.scalar.activation(phi_exp[:, k % 2, :], neg_relu[:, k % 2, :], ACT.Exp,
                                     scale=-1.0).then_inc(phi_exp_ready, 1)

            def f_gelu(g, n):
                bank, drained = filled(F, ("w1", n), g)
                for m in range(2):
                    c = 2 * n + m
                    last = nc.scalar.activation(g_t[:, c, :], bank[:, m * TG:(m + 1) * TG], ACT.Gelu,
                                                bias=cols[:, 8 + c:9 + c])
                last.then_inc(drained, 1)

            def step(gx, gl, gf, gi):
                if gx is not None:
                    bank, drained = filled(X, "ctx", gx)
                    nc.scalar.activation(ctx_t[:], bank[:], ACT.Identity, scale=cols[:, 2:3],
                                         bias=cols[:, 3:4]).then_inc(drained, 1)
                    x_t(gx, 0)
                    x_t(gx, 1)
                for k in range(8):
                    if gx is not None and k + 2 < 8:
                        x_t(gx, k + 2)
                    if gf is not None and k == 4:
                        f_gelu(gf, 0)
                    if gl is not None:
                        l_relu(gl, k)
                    if gf is not None and k == 4:
                        f_gelu(gf, 1)
                    if gl is not None:
                        l_exp(gl, k)
                for j in range(JG):
                    if gx is not None:
                        for b in (2 * j, 2 * j + 1):
                            for c in range(2):
                                x_exp(gx, b, c)
                            for c in range(2):
                                values(X, ("V", b, c), gx, v_x[:, b % 2, 8 * c:8 * c + 8, 0:DH])
                    if gl is not None:
                        for c in range(2):
                            values(L, ("v", j, c), gl, v_l[:, 8 * c:8 * c + 8, 0:DH])
                        for c in range(2):
                            copy_out(L, ("T", j, c), gl, ot_l[:, c * 512:(c + 1) * 512])
                    if gx is not None:
                        for c in range(2):
                            copy_out(X, ("T", j, c), gx, ot_x[:, c * 512:(c + 1) * 512])

            steps(act, step)

            def e_relu(i, r, expert):
                bank, drained = filled(E, ("hA", r), i)
                for c in range(2):
                    last = nc.scalar.activation(hid_t[:, r % 2, c, :], bank[:, c * P:(c + 1) * P], ACT.Relu,
                                                bias=gate_b1_t[:, bass.ds(expert * 4 + (NE + c), 1)])
                last.then_inc(drained, 1)

            def tiles(i, first, last):
                for r in range(RING):
                    expert = act.value_load(expert_of[0:1, bass.ds(RING * i + r, 1)], min_val=0, max_val=NE - 1)
                    e_relu(i, r, expert)

            act.wait_ge(experts_known, 1)
            tile_steps(act, tiles)

        @block.vector
        def _(dve):
            V = nc.vector
            V.memset(v_x[:, :, :, DH:DH + 1], 1.0)
            V.memset(v_l[:, :, DH:DH + 1], 1.0)
            V.memset(minus_half[:], -0.5).then_inc(consts_ready, 1)
            for n in range(1, 8, 2):
                dve.wait_ge(bank_filled[n], 1)
                V.tensor_copy(raw_t[RAW[n // 2]][:, 4:8, :],
                              ps[n][:].rearrange("p (c m) -> p c m", m=P)).then_inc(bank_drained[n], 1)
            for n in range(1, 8, 2):
                dve.wait_ge(bank_filled[n], 2)
                if n < 4:
                    dst = absorbed[:, 8 * (n // 2) + 1:8 * (n // 2) + 8:2, :]
                    src = ps[n][:].rearrange("p (c m) -> p c m", m=P)
                else:
                    dst = (wq_phi if n == 5 else wk_phi)[:].rearrange("p (c h e) -> p c h e", h=2, e=DH)[:, :, 1, :]
                    src = ps[n][:].rearrange("p (c e) -> p c e", e=DH)
                V.tensor_copy(dst, src).then_inc(bank_drained[n], 1)
            dve.wait_ge(bank_filled[7], 3)
            V.tensor_copy(gate_b1_t[:], ps[7][:, 0:5 * NE]).then_inc(bank_drained[7], 1)
            dve.wait_ge(cols_loaded, 16 * NCOLS)
            dve.wait_ge(consts_ready, 2)
            dve.wait_ge(rows_loaded, 16 * NROWS)

            def waits_alone():
                dve.sem_inc(dve_waits_passed, 1)

            class Own:

                def __init__(self, landed, per_group):
                    self.landed, self.per_group, self.n = landed, per_group, 0

                def land(self, g, instruction):
                    self.n += 1
                    instruction.then_inc(self.landed, 1)
                    dve.wait_ge(self.landed, g * self.per_group + self.n)
                    self.n %= self.per_group

            of_in, of_x, of_l = Own(in_step, 2), Own(x_step, 4 * JG + 2 * JG), Own(l_step, 8 * JG + 2 * JG)
            of_f = Own(f_step, 3)

            def filled(stage, name, g):
                bank = stage.bank(name)
                dve.wait_ge(bank_filled[bank], stage.count(name, g) + 1)
                return ps[bank], bank_drained[bank]

            def taken(stage, name, g):
                dve.wait_ge(bank_drained[stage.bank(name)], stage.count(name, g) + 1)

            def var_once(dst, var):
                return V.tensor_scalar(dst, var, EPS, None, ALU.add)

            def var_twice(dst, var):
                return V.tensor_scalar(dst, var, 1.0 + EPS, EPS * EPS, ALU.mult, ALU.add)

            def normalise(dst, src, mv, n, rstd):
                return V.tensor_scalar(dst, src, mv[:, n, 0:1], rstd, ALU.subtract, ALU.mult)

            def in_stats(g):
                if isinstance(g, int) and g == 0:
                    dve.wait_ge(x_loaded, 16)
                else:
                    dve.wait_ge(x_loaded, 32)
                dve.wait_ge(ctx_loaded, 16 * g + 16)
                waits_alone()
                for j in range(JG):
                    V.bn_stats(st_in[:, j, :], state[:, JG * g + j, :])
                for b in range(BG):
                    last = V.bn_stats(st_in[:, JG + b, :], ctx_in[:, b, :])
                of_in.land(g, last)
                waits_alone()
                for n in range(JG + BG):
                    last = V.bn_aggr(mv_in[:, n, :], st_in[:, n, :])
                of_in.land(g, last)
                var_twice(var_in[:, 0:JG], mv_in[:, 0:JG, 1])
                var_once(var_in[:, JG:], mv_in[:, JG:, 1]).then_inc(var_in_ready, 1)

            def in_normalise(g):
                dve.wait_ge(rstd_in_ready, g + 1)
                for j in range(JG):
                    normalise(z_in[:, j, :], state[:, JG * g + j, :], mv_in, j, rstd_in[:, j:j + 1])
                for b in range(BG):
                    n = JG + b
                    last = normalise(z_in[:, n, :], ctx_in[:, b, :], mv_in, n, rstd_in[:, n:n + 1])
                last.then_inc(z_in_ready, 1)

            def affine_out(stage, name, g, dst, col):
                bank, drained = filled(stage, name, g)
                V.tensor_scalar(dst, bank[:, 0:TG], cols[:, col:col + 1], cols[:, col + 1:col + 2],
                                ALU.mult, ALU.add).then_inc(drained, 1)

            def l_phi(g, k):
                bank, drained = filled(L, ("qk", k), g)
                dve.wait_ge(phi_exp_ready, g * 8 + (k + 1))
                dst = (q_t if k < 4 else k_t)[:, 2 * (k % 4):2 * (k % 4) + 2, :]
                V.scalar_tensor_tensor(out=dst.rearrange("p a b -> p (a b)"), in0=bank[:], scalar=0.0,
                                       in1=phi_exp[:, k % 2, :], op0=ALU.max, op1=ALU.add)\
                 .then_inc(drained, 1)

            def x_clip(g, b, c):
                n = 2 * b + c
                if n % 4 >= 2:
                    dve.wait_ge(probs_ready, g * (2 * BG) + (n - 1))
                bank, drained = filled(X, ("S", b, c), g)
                V.tensor_scalar(clipped[:, n % 2, :], bank[:], -CLIP / SCALE, CLIP / SCALE,
                                ALU.max, ALU.min).then_inc(drained, 1)

            def l_mask(g, j, par):
                bank, drained = filled(L, ("A", j, par), g)
                V.tensor_tensor(a_t[:, par, :, :], bank[:].rearrange("p (c t) -> p c t", t=NL),
                                causal[:].unsqueeze(1).to_broadcast([P, 8, NL]), ALU.mult).then_inc(drained, 1)

            def divide_heads(stage, name, g, dst, q, own, eps):
                bank, drained = filled(stage, name, g)
                heads = bank[:, 0:4 * (DH + 1)].rearrange("p (h e) -> p h e", e=DH + 1)
                d, r = den[:, q % 2, :], rden[:, q % 2, :]
                if eps:
                    own.land(g, V.tensor_scalar(d, heads[:, :, DH], eps, None, ALU.add))
                    own.land(g, V.reciprocal(r, d))
                else:
                    own.land(g, V.reciprocal(r, heads[:, :, DH]))
                V.tensor_tensor(dst[:, q * 256:(q + 1) * 256].rearrange("p (h e) -> p h e", e=DH),
                                heads[:, :, 0:DH], r.unsqueeze(2).to_broadcast([P, 4, DH]),
                                ALU.mult).then_inc(drained, 1)

            def pair_stats(g, j, src, st, mv, own):
                waits_alone()
                own.land(g, V.bn_stats(st[:, j, :], src))
                waits_alone()
                own.land(g, V.bn_aggr(mv[:, j, :], st[:, j, :]))

            def l_finish(g, j):
                bank, drained = filled(L, ("wo", j), g)
                V.tensor_tensor(zf[:, j, :], bank[:, 0:D], z_res[:, j, :], ALU.add).then_inc(drained, 1)
                taken(L, ("wo", j), g)
                pair_stats(g, j, zf[:, j, :], st_z, mv_z, of_l)

            def x_finish(g, j):
                bank, drained = filled(X, ("Wo", j), g)
                dve.wait_ge(bo_added, g * JG + (j + 1))
                V.tensor_tensor(state[:, JG * g + j, :], bank[:, 0:D], x_plus_bo[:, j, :], ALU.add)\
                 .then_inc(drained, 1)
                taken(X, ("Wo", j), g)
                pair_stats(g, j, state[:, JG * g + j, :], st_x1, mv_x1, of_x)

            def f_finish(g):
                bank, drained = filled(F, "w2", g)
                dve.wait_ge(b2_added, g * JG + JG)
                V.tensor_tensor(f_sum[:], bank[:, 0:JG * D].rearrange("p (j d) -> p j d", d=D), zf_b2[:],
                                ALU.add).then_inc(drained, 1)
                taken(F, "w2", g)
                here = records[:, bass.ds(JG * g, JG), D:2 * D]
                of_f.land(g, V.tensor_tensor(here, state[:, bass.ds(JG * g, JG), :], f_sum[:], ALU.add))
                waits_alone()
                for j in range(JG):
                    last = V.bn_stats(st_r[:, j, :], records[:, JG * g + j, D:2 * D])
                of_f.land(g, last)
                waits_alone()
                for j in range(JG):
                    last = V.bn_aggr(mv_r[:, j, :], st_r[:, j, :])
                of_f.land(g, last)
                var_once(var_r[:], mv_r[:, :, 1]).then_inc(var_r_ready, 1)

            def r_normalise(g):
                dve.wait_ge(rstd_r_ready, g + 1)
                for j in range(JG):
                    x2 = records[:, JG * g + j, D:2 * D]
                    normalise(records[:, JG * g + j, 0:D], x2, mv_r, j, rstd_r[:, j:j + 1])
                    last = normalise(z_r[:, j, :], x2, mv_r, j, rstd_r[:, j:j + 1])
                last.then_inc(z_r_ready, 1)

            def r_logits(g):
                bank, drained = filled(F, "zr", g)
                V.tensor_copy(zr_t[:], bank[:, 0:TG]).then_inc(drained, 1)
                bank, drained = filled(F, "gate", g)
                V.tensor_tensor(logits[:, bass.ds(JG * g, JG), :],
                                bank[:, 0:JG * NE].rearrange("p (j e) -> p j e", e=NE),
                                gate_b_row[:].unsqueeze(1).to_broadcast([P, JG, NE]), ALU.add).then_inc(drained, 1)

            def step(gx, gl, gf, gi):
                if gx is not None:
                    affine_out(X, "lat", gx, lat_t[:], 0)
                if gl is not None:
                    affine_out(L, "h", gl, h_t[:], 4)
                if gf is not None:
                    affine_out(F, "h", gf, f_t[:], 6)
                for k in range(8):
                    if gl is not None:
                        l_phi(gl, k)
                    if gi is not None and k == 2:
                        in_stats(gi)
                    if gi is not None and k == 5:
                        dve.wait_ge(bank_filled[X.bank("ctx")], X.count("ctx", gx) + 1)
                        in_normalise(gi)
                if gf is not None:
                    f_finish(gf)
                for j in range(JG):
                    if gx is not None:
                        for b in (2 * j, 2 * j + 1):
                            for c in range(2):
                                x_clip(gx, b, c)
                    if gf is not None and j == 0:
                        r_normalise(gf)
                    if gl is not None:
                        for par in range(2):
                            l_mask(gl, j, par)
                        for q in range(4):
                            divide_heads(L, ("AV", j, q), gl, o_l, q, of_l, 1e-6)
                    if gx is not None:
                        for q in range(4):
                            divide_heads(X, ("PV", j, q), gx, o_x, q, of_x, None)
                    if gl is not None:
                        l_finish(gl, j)
                    if gx is not None:
                        x_finish(gx, j)
                    if gf is not None and j == 0:
                        r_logits(gf)
                if gl is not None:
                    var_once(var_z[:], mv_z[:, :, 1]).then_inc(var_z_ready, 1)
                if gx is not None:
                    var_once(var_x1[:, 0, :], mv_x1[:, :, 1])
                    var_twice(var_x1[:, 1, :], mv_x1[:, :, 1]).then_inc(var_x1_ready, 1)
                if gl is not None:
                    dve.wait_ge(rstd_z_ready, gl + 1)
                    for j in range(JG):
                        last = normalise(f_z[:, j, :], zf[:, j, :], mv_z, j, rstd_z[:, j:j + 1])
                    last.then_inc(f_z_ready, 1)
                if gx is not None:
                    dve.wait_ge(rstd_x1_ready, gx + 1)
                    for j in range(JG):
                        x1 = state[:, JG * gx + j, :]
                        normalise(z_res[:, j, :], x1, mv_x1, j, rstd_x1[:, 0, j:j + 1])
                        last = normalise(h_z[:, j, :], x1, mv_x1, j, rstd_x1[:, 1, j:j + 1])
                    last.then_inc(h_z_ready, 1)

            in_stats(0)
            in_normalise(0)
            steps(dve, step)

            of_route = Own(route_step, 1 << 30)

            def now(instruction):
                of_route.land(0, instruction)

            def by_tile(tile):
                return tile[:].rearrange("p (t e) -> p t e", e=NE)

            def over_tiles(row):
                return row.unsqueeze(1).to_broadcast([P, NT, NE])

            w = [by_tile(t) for t in work]
            taken(F, "gate", NG - 1)
            now(V.tensor_tensor(logits[:], logits[:], over_tiles(expert_bias_row[:]), ALU.add))
            now(V.tensor_reduce(best[:, 0, :], logits[:], AX.X, ALU.max))
            now(V.tensor_tensor(w[0], logits[:], best[:, 0, :].unsqueeze(2).to_broadcast([P, NT, NE]), ALU.is_ge))
            now(V.scalar_tensor_tensor(out=w[1], in0=w[0], scalar=-float(NE), in1=over_tiles(iota_e[:]),
                                       op0=ALU.mult, op1=ALU.add))
            now(V.tensor_reduce(best[:, 1, :], w[1], AX.X, ALU.min))
            V.tensor_tensor(chosen[:], over_tiles(expert_m8[:]), best[:, 1, :].unsqueeze(2).to_broadcast([P, NT, NE]),
                            ALU.is_equal).then_inc(chosen_ready, 1)
            bank, drained = filled(R, "rank", 0)
            totals = bank[:, NT * NE:2 * NT * NE].rearrange("p (t e) -> p t e", e=NE)
            now(V.tensor_copy(w[0], totals))
            a, b, reach = w[0], w[1], 1
            while reach < NT:
                V.tensor_copy(b[:, 0:reach, :], a[:, 0:reach, :])
                now(V.tensor_tensor(b[:, reach:, :], a[:, reach:, :], a[:, 0:NT - reach, :], ALU.add))
                a, b, reach = b, (w[2] if b is w[1] else w[1]), 2 * reach
            counts = a[:, NT - 1, :]
            now(V.tensor_tensor(w[3].rearrange("p t e -> p e t"), counts.unsqueeze(2).to_broadcast([P, NE, NT]),
                                thresholds[:].unsqueeze(1).to_broadcast([P, NE, NT]), ALU.is_gt))
            now(V.tensor_reduce(tiles_of[:, 0, :], w[3].rearrange("p t e -> p e t"), AX.X, ALU.add))
            now(V.tensor_tensor(earlier_expert[:], earlier_expert[:],
                                tiles_of[:, 0, :].unsqueeze(1).to_broadcast([P, NE, NE]), ALU.mult))
            now(V.tensor_reduce(tiles_of[:, 1, :], earlier_expert[:], AX.X, ALU.add))
            now(V.tensor_tensor(tiles_of[:, 2, :], tiles_of[:, 0, :], tiles_of[:, 1, :], ALU.add))
            ends = tile_ends[0:1, :, :]
            now(V.tensor_tensor(ends, tiles_of[0:1, 2, :].unsqueeze(1).to_broadcast([1, NS, NE]),
                                tile_no[0:1, :].unsqueeze(2).to_broadcast([1, NS, NE]), ALU.is_le))
            now(V.tensor_reduce(per_tile[0:1, :], ends, AX.X, ALU.add))
            V.tensor_scalar(expert_of[0:1, :], per_tile[0:1, :], float(NE - 1), None, ALU.min).then_inc(experts_known, 1)
            now(V.tensor_tensor(a, a, w[0], ALU.subtract))
            V.tensor_tensor(b, bank[:, 0:NT * NE].rearrange("p (t e) -> p t e", e=NE), a, ALU.add).then_inc(drained, 1)
            taken(R, "rank", 0)
            now(V.scalar_tensor_tensor(out=w[3], in0=over_tiles(tiles_of[:, 1, :]), scalar=float(P), in1=b,
                                       op0=ALU.mult, op1=ALU.add))
            now(V.tensor_tensor(w[3], w[3], chosen[:], ALU.mult))
            now(V.tensor_reduce(best[:, 0, :], w[3], AX.X, ALU.add))
            V.tensor_copy(slot_of[:], best[:, 0, :]).then_inc(slots_known, 1)

            def e_inputs(i, r, expert):
                bank, drained = filled(E, ("z", r), i)
                V.tensor_copy(w1_now[:, r % 2, :], e_w1[:, expert, :]).then_inc(w1_now_ready, 1)
                V.tensor_copy(slot_t[:, r % 2, :], bank[:, 0:P]).then_inc(drained, 1)

            def e_relu(i, r, expert):
                bank, drained = filled(E, ("hB", r), i)
                for m in range(2):
                    b1 = gate_b1_t[:, bass.ds(expert * 4 + (NE + 2 + m), 1)]
                    last = V.tensor_scalar(hid_t[:, r % 2, 2 + m, :], bank[:, m * P:(m + 1) * P], b1, 0.0,
                                           ALU.add, ALU.max)
                last.then_inc(drained, 1)

            def e_finish(i, r, expert):
                V.tensor_tensor(x2_b2[:, r % 2, :], slot_in[:, r, D:2 * D], e_b2[:, bass.ds(expert * D, D)],
                                ALU.add).then_inc(b2_ready, 1)
                dve.wait_ge(b2_ready, RING * i + (r + 1))
                bank, drained = filled(E, ("y", r), i)
                V.tensor_tensor(slot_out[:, r, :], bank[:, 0:D], x2_b2[:, r % 2, :], ALU.add).then_inc(drained, 1)

            def tiles(i, first, last):
                def expert(n):
                    return dve.value_load(expert_of[0:1, bass.ds(n, 1)], min_val=0, max_val=NE - 1)
                experts = {r: expert(RING * i + r) for r in range(-1, RING + 1)
                           if not (first and r < 0) and not (last and r == RING)}
                if first:
                    e_inputs(i, 0, experts[0])
                for r in range(RING):
                    if r + 1 < RING:
                        e_inputs(i, r + 1, experts[r + 1])
                    elif not last:
                        e_inputs(i + 1, 0, experts[RING])
                    e_relu(i, r, experts[r])
                    if r > 0:
                        e_finish(i, r - 1, experts[r - 1])
                    elif not first:
                        e_finish(i - 1, RING - 1, experts[-1])
                if last:
                    e_finish(i, RING - 1, experts[RING - 1])

            dve.wait_ge(experts_known, 1)
            dve.wait_ge(e_w1_loaded, 16)
            tile_steps(dve, tiles)

        @block.gpsimd
        def _(pool):
            G = nc.gpsimd
            G.memset(ident[:], 0.0).then_inc(ident_zeroed, 1)
            G.memset(causal[:], 1.0).then_inc(ident_zeroed, 1)
            pool.dma_start(bo_row[:], wts["bo"].partition_broadcast(P)).then_inc(rows_loaded, 16)
            pool.dma_start(b2_row[:], wts["b2"].partition_broadcast(P)).then_inc(rows_loaded, 16)
            pool.dma_start(gate_b_row[:], wts["gate_b"].partition_broadcast(P)).then_inc(rows_loaded, 16)
            pool.dma_start(expert_bias_row[:], wts["expert_bias"].partition_broadcast(P)).then_inc(rows_loaded, 16)
            pool.dma_start(e_b2[:], wts["e_b2"].rearrange("e d -> (e d)").partition_broadcast(P)).then_inc(rows_loaded, 16)
            pool.wait_ge(ident_zeroed, 2)
            for half in range(2):
                part = causal[half * NL:(half + 1) * NL, :]
                G.affine_select(out=part, in_=part, compare_op=ALU.is_ge, fill=0.0, base=0,
                                pattern=[[1, NL]], channel_multiplier=-1).then_inc(causal_half, 1)
                pool.wait_ge(causal_half, half + 1)
            G.affine_select(out=ident[:], in_=ident[:], compare_op=ALU.not_equal, fill=1.0, base=0,
                            pattern=[[-1, P]], channel_multiplier=1).then_inc(consts_ready, 1)
            G.memset(empty_record[:], 0.0).then_inc(empty_ready, 1)
            pool.wait_ge(empty_ready, 1)
            G.iota(empty_record[:, 2 * D:REC].bitcast(U32), pattern=[[0, 1]], base=NOBODY,
                   channel_multiplier=0).then_inc(empty_ready, 1)
            pool.wait_ge(empty_ready, 2)
            G.iota(records[:, :, 2 * D:REC].bitcast(U32), pattern=[[P, NT], [0, 1]], base=0, channel_multiplier=1)
            for tile, start, stride in ((expert_m8, -NE, 1), (iota_e, 0, 1), (thresholds, 0, P), (tile_no, 0, 1)):
                G.iota(tile[:], pattern=[[stride, tile.shape[1]]], base=start, channel_multiplier=0,
                       allow_small_or_imprecise_dtypes=True)
            G.memset(ones[:], 1.0)
            G.memset(earlier_row[:], 1.0)
            G.memset(earlier_expert[:], 1.0).then_inc(empty_ready, 1)
            pool.wait_ge(empty_ready, 3)
            G.affine_select(out=earlier_row[:], in_=earlier_row[:], compare_op=ALU.is_ge, fill=0.0, base=-1,
                            pattern=[[1, P]], channel_multiplier=-1)
            G.affine_select(out=earlier_expert[:], in_=earlier_expert[:], compare_op=ALU.is_ge, fill=0.0, base=-1,
                            pattern=[[1, NE], [-1, NE]], channel_multiplier=0).then_inc(routing_consts, 1)
            pool.wait_ge(routing_consts, 1)
            pool.wait_ge(consts_ready, 2)
            pool.wait_ge(rows_loaded, 16 * NROWS)

            def power(var, rstd, ready, powered, g, n):
                pool.wait_ge(ready, g + 1)
                G.tensor_tensor(rstd, var, minus_half[:, 0:n], ALU.pow).then_inc(powered, 1)

            def taken(stage, name, g):
                pool.wait_ge(bank_drained[stage.bank(name)], stage.count(name, g) + 1)

            def step(gx, gl, gf, gi):
                if gx is not None:
                    if isinstance(gx, int) and gx == 0:
                        pool.wait_ge(x_loaded, 16)
                    else:
                        pool.wait_ge(x_loaded, 32)
                    for j in range(JG):
                        if not (isinstance(gx, int) and gx == 0):
                            taken(X, ("Wo", j), gx - 1)
                        G.tensor_tensor(x_plus_bo[:, j, :], state[:, JG * gx + j, :], bo_row[:],
                                        ALU.add).then_inc(bo_added, 1)
                if gi is not None:
                    power(var_in[:], rstd_in[:], var_in_ready, rstd_in_ready, gi, JG + BG)
                if gf is not None:
                    power(var_r[:], rstd_r[:], var_r_ready, rstd_r_ready, gf, JG)
                if gl is not None:
                    for j in range(JG):
                        taken(L, ("wo", j), gl)
                        G.tensor_tensor(zf_b2[:, j, :], zf[:, j, :], b2_row[:], ALU.add).then_inc(b2_added, 1)
                    power(var_z[:], rstd_z[:], var_z_ready, rstd_z_ready, gl, JG)
                if gx is not None:
                    power(var_x1[:].rearrange("p a j -> p (a j)"), rstd_x1[:].rearrange("p a j -> p (a j)"),
                          var_x1_ready, rstd_x1_ready, gx, 2 * JG)

            power(var_in[:], rstd_in[:], var_in_ready, rstd_in_ready, 0, JG + BG)
            steps(pool, step)

            pool.wait_ge(slots_emptied, 16)
            pool.wait_ge(slots_known, 1)
            pool.wait_ge(z_r_ready, NG)
            for t in range(NT):
                pool.indirect_dma_start(slots, bass.IndirectOffsetOnAxis(ap=slot_of[:, t:t + 1], axis=0),
                                        records[:, t, :], None).then_inc(slots_written, 16)

            def tiles(i, first, last):
                for r in range(RING):
                    pool.wait_ge(bank_drained[E.bank(("y", r))], E.count(("y", r), i) + 1)
                    pool.sem_inc(pool_waits_passed, 1)
                    pool.indirect_dma_start(
                        out_rows, bass.IndirectOffsetOnAxis(ap=slot_in[:, r, 2 * D:REC].bitcast(U32), axis=0),
                        slot_out[:, r, :], None, bounds_check=NB * NL - 1, oob_is_err=False)\
                        .then_inc(tokens_written[r], 16)

            tile_steps(pool, tiles)


_WEIGHTS = {
    "ln_l_w": "L0_xattn_ln_l_w", "ln_l_b": "L0_xattn_ln_l_b", "ln_c_w": "L0_xattn_ln_c_w",
    "ln_c_b": "L0_xattn_ln_c_b", "Wq": "L0_xattn_Wq", "Wkv": "L0_xattn_Wkv", "Wo": "L0_xattn_Wo",
    "bo": "L0_xattn_bo", "wq": "L0_attn_wq", "wk": "L0_attn_wk", "wv": "L0_attn_wv", "wo": "L0_attn_wo",
    "proj": "L0_attn_proj", "w1": "L0_attn_w1", "b1": "L0_attn_b1", "w2": "L0_attn_w2", "b2": "L0_attn_b2",
    "g1": "L0_attn_g1", "beta1": "L0_attn_beta1", "g2": "L0_attn_g2", "beta2": "L0_attn_beta2",
    "gate_w": "L0_ffn_gate_w", "gate_b": "L0_ffn_gate_b", "expert_bias": "L0_ffn_expert_bias",
    "e_w1": "L0_ffn_w1", "e_b1": "L0_ffn_b1", "e_w2": "L0_ffn_w2", "e_b2": "L0_ffn_b2",
}


def kernel(**inputs):
    import numpy as _np
    import concourse.bacc as _bacc
    from concourse import mybir as _mybir
    from concourse.bass_utils import run_bass_kernel_spmd as _run

    nc = _bacc.Bacc("TRN2", target_bir_lowering=False, num_devices=1)
    arrays = {}

    def dram(name):
        a = _np.ascontiguousarray(inputs[name])
        arrays[f"in_{name}_dram"] = a
        return nc.dram_tensor(f"in_{name}_dram", a.shape, _mybir.dt.from_np(a.dtype), kind="ExternalInput").ap()

    x, ctx = dram("x"), dram("ctx_1024")
    wts = {short: dram(name) for short, name in _WEIGHTS.items()}
    out = nc.dram_tensor("out_0_dram", inputs["x"].shape, _mybir.dt.float32, kind="ExternalOutput").ap()
    slots = nc.dram_tensor("slots_dram", (NS * P, REC), _mybir.dt.float32, kind="Internal").ap()
    perceiver_layer(nc, x, ctx, wts, out, slots)
    r = _run(nc, [arrays], core_ids=[0])
    return r.results[0]["out_0_dram"]
```

```python
import concourse.bass as bass
from concourse import mybir
from contextlib import ExitStack

NB, NL, D = 32, 64, 128
NC = 128
H, DH = 16, 64
INNER = H * DH
FF = 512
NE = 8
P = 128
NG = NB // 2
BG = NB // NG
LAG = 4
NT = NB * NL // P
RING = 4
NS = -(-(NT + NE - 1) // RING) * RING
REC = 2 * D + 1
NOBODY = 2 * NB * NL - 1
EPS = 1e-5
SCALE = DH ** -0.5
CLIP = 11.0


class Banks:

    def __init__(self, first, number, chunks, before):
        self.place = {c: (first + n % number, n // number) for n, c in enumerate(chunks)}
        self.uses = {first + m: len(range(m, len(chunks), number)) for m in range(number)}
        self.before = dict.fromkeys(self.uses, before) if isinstance(before, int) else before

    def bank(self, chunk):
        return self.place[chunk][0]

    def count(self, chunk, g):
        bank, use = self.place[chunk]
        return g * self.uses[bank] + (self.before[bank] + use)

    def after(self, pairs):
        return {bank: self.before[bank] + pairs * uses for bank, uses in self.uses.items()}

    def needs(self, chunk, reads, g):
        last = {}
        for bank, uses in [self.place[chunk]] + [(self.place[c][0], self.place[c][1] + 1) for c in reads]:
            last[bank] = max(uses, last.get(bank, 0))
        return [(bank, g * self.uses[bank] + (self.before[bank] + uses)) for bank, uses in last.items()]


def perceiver_layer(nc, x, ctx, wts, out, slots):
    F32 = mybir.dt.float32
    F32R = mybir.dt.float32r
    U32 = mybir.dt.uint32
    I32 = mybir.dt.int32
    AX = mybir.AxisListType
    ALU = mybir.AluOpType
    ACT = mybir.ActivationFunctionType

    x_v = x.rearrange("b n d -> (b n) d").rearrange("(g p) d -> g p d", p=P)
    out_rows = out.rearrange("b n d -> (b n) d")
    slots_v = slots.rearrange("(n p) c -> n p c", p=P)
    ctx_v = ctx.rearrange("(g b) s d -> g s b d", b=BG)

    XF = Banks(0, 2, ["lat", "ctx"] + [("t", k) for k in range(4)]
               + [("S", 0, 0), ("V", 0, 0), ("V", 0, 1), ("S", 0, 1), ("S", 1, 0), ("V", 1, 0),
                  ("S", 1, 1), ("V", 1, 1)], 2)
    XB = Banks(2, 1, [("heads", q) for q in range(4)] + [("T", 0), ("T", 1), "out"], 2)
    LF = Banks(3, 2, ["h"] + [("qk", k) for k in range(4)] + [("A", 0), ("v", 0), ("A", 1), ("v", 1)], 2)
    LB = Banks(5, 2, [("heads", q) for q in range(4)] + [("T", 0), ("T", 1), "out"], 2)
    F = Banks(7, 1, ["h", "w1", "w2", "zr", "gate"], 3)
    R = Banks(7, 1, ["rank"], F.after(NG))
    E = Banks(0, 8, [(n, r) for r in range(RING) for n in ("z", "hA", "hB", "y")],
              {**XF.after(NG), **XB.after(NG), **LF.after(NG), **LB.after(NG), **R.after(1)})

    es = ExitStack()
    with es:
        def sb(name, shape, dt=F32):
            return es.enter_context(nc.sbuf_tensor(name, shape, dt))

        def sem(name):
            return es.enter_context(nc.semaphore(name))

        ident = sb("ident", [P, P])
        causal = sb("causal", [P, NL])
        minus_half = sb("minus_half", [P, 8])
        zero, exp_of_zero = sb("zero", [P, 1]), sb("exp_of_zero", [P, 1])
        attn_weights = sb("attn_weights", [P, H * P + 4 * INNER])
        absorbed = attn_weights[:, 0:H * P].rearrange("p (h d) -> p h d", h=H)
        wo_x, wq_phi, wk_phi, wo_l = (
            attn_weights[:, H * P + n * INNER:H * P + (n + 1) * INNER] for n in range(4))
        wo_x, wo_l = (w.rearrange("p (c n) -> p c n", n=P) for w in (wo_x, wo_l))
        wv_hi, wv_lo = (sb(f"wv_{part}", [P, 2, INNER], F32R) for part in ("hi", "lo"))
        w1 = sb("w1", [P, FF])
        w2 = sb("w2", [P, 4, P])
        proj2 = sb("proj2", [P, DH])
        cols = sb("cols", [P, 12])
        bo_row = sb("bo_row", [P, D])
        b2_row = sb("b2_row", [P, D])
        state = sb("state", [P, NB // 2, D])
        ctx_in = sb("ctx_in", [P, BG, D])
        z_in = sb("z_in", [P, 1 + BG, D])
        lat_t = sb("lat_t", [P, P])
        ctx_t = sb("ctx_t", [P, BG * NC])
        ctx_hi, ctx_lo = (sb(f"ctx_{part}", [P, BG * NC], F32R) for part in ("hi", "lo"))
        t_hi, t_lo = (sb(f"t_{part}", [P, H, P], F32R) for part in ("hi", "lo"))
        clipped = sb("clipped", [P, 2, 512])
        probs = sb("probs", [P, BG, H * NL])
        v_x = sb("v_x", [P, BG, H, DH + 1])
        o_x = sb("o_x", [P, INNER])
        ot_x = sb("ot_x", [P, INNER])
        x_plus_bo = sb("x_plus_bo", [P, D])
        h_z = sb("h_z", [P, D])
        h_t = sb("h_t", [P, P])
        h_hi, h_lo = (sb(f"h_{part}", [P, P], F32R) for part in ("hi", "lo"))
        qk_t = sb("qk_t", [P, 16, P])
        q_t, k_t = qk_t[:, 0:8, :], qk_t[:, 8:16, :]
        neg_relu = sb("neg_relu", [P, 2, 512])
        phi_exp = sb("phi_exp", [P, 2, 512])
        v_l = sb("v_l", [P, H, DH + 1])
        a_t = sb("a_t", [P, 2, 8, NL])
        o_l = sb("o_l", [P, INNER])
        ot_l = sb("ot_l", [P, INNER])
        zf = sb("zf", [P, D])
        zf_b2 = sb("zf_b2", [P, D])
        f_z = sb("f_z", [P, D])
        f_t = sb("f_t", [P, P])
        g_t = sb("g_t", [P, 4, P])
        f_sum = sb("f_sum", [P, D])
        records = sb("records", [P, NT, REC])
        z_r = sb("z_r", [P, D])
        zr_t = sb("zr_t", [P, P])
        gate_in = sb("gate_in", [NE, D])
        b1_in = sb("b1_in", [NE * 4, P])
        gate_b1_t = sb("gate_b1_t", [P, NE + NE * 4])
        gate_b_row = sb("gate_b_row", [P, NE])
        expert_bias_row = sb("expert_bias_row", [P, NE])
        logits = sb("logits", [P, NT, NE])
        expert_m8 = sb("expert_m8", [P, NE])
        thresholds = sb("thresholds", [P, NT])
        tile_no = sb("tile_no", [P, NS])
        earlier_expert = sb("earlier_expert", [P, NE, NE])
        earlier_row = sb("earlier_row", [P, P])
        ones = sb("ones", [P, P])
        iota_e = sb("iota_e", [P, NE])
        tile_ends = sb("tile_ends", [1, NS, NE])
        work = [sb(f"work{n}", [P, NT * NE]) for n in range(4)]
        chosen = sb("chosen", [P, NT, NE])
        best = sb("best", [P, 2, NT])
        tiles_of = sb("tiles_of", [P, 3, NE])
        per_tile = sb("per_tile", [1, 1 + NS + 1])
        packed = sb("packed", [1, 2, NS // RING])
        experts_of = sb("experts_of", [1, NS // RING], I32)
        slot_of = sb("slot_of", [P, NT], U32)
        empty_record = sb("empty_record", [P, REC])
        st_r = sb("st_r", [P, 6])
        mv_r = sb("mv_r", [P, 2])
        var_r = sb("var_r", [P, 1])
        rstd_r = sb("rstd_r", [P, 1])
        e_w1 = sb("e_w1", [P, NE, FF])
        e_w2 = sb("e_w2", [P, NE * 4, D])
        slot_z = o_l[:, 0:RING * D].rearrange("p (r d) -> p r d", d=D)
        slot_rest = attn_weights[:, 0:NS * (REC - D)].rearrange("p (n c) -> p n c", c=REC - D)
        e_b2 = sb("e_b2", [P, NE * D])
        slot_t = ot_l[:, 0:2 * P].rearrange("p (r n) -> p r n", n=P)
        w1_now = o_x[:].rearrange("p (r f) -> p r f", f=FF)
        hid_t = ot_x[:].rearrange("p (r c n) -> p r c n", r=2, n=P)
        x2_b2 = ot_l[:, 2 * P:2 * P + 2 * D].rearrange("p (r d) -> p r d", d=D)
        token_no = sb("token_no", [P, RING], U32)
        slot_out = o_l[:, RING * D:2 * RING * D].rearrange("p (r d) -> p r d", d=D)
        st_in = sb("st_in", [P, 1 + BG, 6])
        mv_in = sb("mv_in", [P, 1 + BG, 2])
        var_in = sb("var_in", [P, 1 + BG])
        rstd_in = sb("rstd_in", [P, 1 + BG])
        st_x1 = sb("st_x1", [P, 6])
        mv_x1 = sb("mv_x1", [P, 2])
        var_x1 = sb("var_x1", [P, 2])
        rstd_x1 = sb("rstd_x1", [P, 2])
        st_z = sb("st_z", [P, 6])
        mv_z = sb("mv_z", [P, 2])
        var_z = sb("var_z", [P, 1])
        rstd_z = sb("rstd_z", [P, 1])
        den_l = sb("den_l", [P, 2, 4])
        rden_x, rden_l = sb("rden_x", [P, 2, 4]), sb("rden_l", [P, 2, 4])

        ps = [es.enter_context(nc.psum_tensor(f"bank{n}", [P, 512], F32)) for n in range(8)]

        raw = {n: e_w1[:, 2 * k:2 * k + 2, :].rearrange("p a b -> p (a b)")
               for k, n in enumerate(("Wq", "Wk", "wq", "wk"))}
        raw_t = {n: e_w2[:, 8 * k:8 * k + 8, :] for k, n in enumerate(("Wq", "Wk", "wq", "wk"))}

        wv_raw = probs

        bank_filled = [sem(f"bank_filled{n}") for n in range(8)]
        bank_drained = [sem(f"bank_drained{n}") for n in range(8)]
        ident_zeroed = sem("ident_zeroed")
        causal_half = sem("causal_half")
        consts_ready = sem("consts_ready")
        rows_loaded = sem("rows_loaded")
        raw_loaded = sem("raw_loaded")
        weights_loaded = sem("weights_loaded")
        wv_split, ctx_split, h_split = sem("wv_split"), sem("ctx_split"), sem("h_split")
        t_hi_ready, h_hi_ready = sem("t_hi_ready"), sem("h_hi_ready")
        table_in = sem("table_in")
        cols_loaded = sem("cols_loaded")
        x_first_loaded, x_loaded = sem("x_first_loaded"), sem("x_loaded")
        ctx_loaded = sem("ctx_loaded")
        pe_waits_passed, dve_waits_passed = sem("pe_waits_passed"), sem("dve_waits_passed")
        pool_waits_passed = sem("pool_waits_passed")
        in_step, x_step, l_step = sem("in_step"), sem("x_step"), sem("l_step")
        var_in_ready, rstd_in_ready = sem("var_in_ready"), sem("rstd_in_ready")
        var_x1_ready, rstd_x1_ready = sem("var_x1_ready"), sem("rstd_x1_ready")
        var_z_ready, rstd_z_ready = sem("var_z_ready"), sem("rstd_z_ready")
        z_in_ready = sem("z_in_ready")
        h_z_ready = sem("h_z_ready")
        f_z_ready = sem("f_z_ready")
        probs_ready = sem("probs_ready")
        relu_ready, phi_exp_ready = sem("relu_ready"), sem("phi_exp_ready")
        bo_added = sem("bo_added")
        b2_added = sem("b2_added")
        var_r_ready, rstd_r_ready = sem("var_r_ready"), sem("rstd_r_ready")
        z_r_ready = sem("z_r_ready")
        f_step, route_step = sem("f_step"), sem("route_step")
        empty_ready = sem("empty_ready")
        routing_consts = sem("routing_consts")
        slots_emptied = sem("slots_emptied")
        e_w1_loaded, e_w2_loaded = sem("e_w1_loaded"), sem("e_w2_loaded")
        chosen_ready = sem("chosen_ready")
        experts_known, slots_known = sem("experts_known"), sem("slots_known")
        slots_written = sem("slots_written")
        z_loaded = [sem(f"z_loaded{r}") for r in range(RING)]
        rest_loaded = [sem(f"rest_loaded{r}") for r in range(RING)]
        w1_now_ready = sem("w1_now_ready")
        b2_ready = sem("b2_ready")
        tokens_written = [sem(f"tokens_written{r}") for r in range(RING)]

        RAW = ("Wq", "Wk", "wq", "wk")
        NRAW, NWTS, NCOLS, NROWS = 8, 6, 12, 5

        block = es.enter_context(nc.Block())

        def steps(engine, step):
            def pairs(s):
                return [s - lag if 0 <= s - lag < NG else None for lag in range(LAG + 1)] \
                    + [s + 1 if s + 1 < NG else None]
            for s in range(LAG):
                step(*pairs(s))
            with engine.Fori(LAG, NG - 1) as s:
                step(s, s - 1, s - 2, s - 3, s - 4, s + 1)
            for s in range(NG - 1, NG + LAG):
                step(*pairs(s))

        def on(g, work, *args):
            if g is not None:
                work(g, *args)

        def experts_near(engine, i):
            packed = engine.value_load(experts_of[0:1, bass.ds(i, 1)], min_val=0, max_val=NE ** (RING + 2) - 1)
            return lambda r: (packed >> (3 * (r + 1))) & (NE - 1)

        def tile_steps(engine, tiles):
            tiles(0, True, False)
            with engine.Fori(1, NS // RING - 1) as i:
                tiles(i, False, False)
            tiles(NS // RING - 1, False, True)

        @block.sync
        def _(sp):
            sp.dma_start(state[:, 0, :], x_v[0]).then_inc(x_first_loaded, 16)
            sp.dma_start(ctx_in[:], ctx_v[0]).then_inc(ctx_loaded, 16)
            sp.dma_start(raw["Wq"], wts["Wq"]).then_inc(raw_loaded, 16)
            sp.dma_start(raw["Wk"], wts["Wkv"][:, 0:INNER]).then_inc(raw_loaded, 16)
            sp.dma_start(raw["wq"], wts["wq"]).then_inc(raw_loaded, 16)
            sp.dma_start(raw["wk"], wts["wk"]).then_inc(raw_loaded, 16)
            for half in range(2):
                sp.dma_start(proj2[half * DH:(half + 1) * DH, :], wts["proj"]).then_inc(raw_loaded, 16)
            sp.dma_start(gate_in[:], wts["gate_w"]).then_inc(raw_loaded, 16)
            sp.dma_start(b1_in[:], wts["e_b1"].rearrange("e f -> (e f)").rearrange("(k p) -> k p", p=P))\
              .then_inc(raw_loaded, 16)
            sp.dma_start(wv_raw[:, 0, :], wts["Wkv"][:, INNER:2 * INNER]).then_inc(weights_loaded, 16)
            sp.dma_start(wo_x[:], wts["Wo"].rearrange("(c p) n -> p c n", p=P)).then_inc(weights_loaded, 16)
            sp.dma_start(wv_raw[:, 1, :], wts["wv"]).then_inc(weights_loaded, 16)
            sp.dma_start(wo_l[:], wts["wo"].rearrange("(c p) n -> p c n", p=P)).then_inc(weights_loaded, 16)
            sp.dma_start(w1[:], wts["w1"]).then_inc(weights_loaded, 16)
            sp.dma_start(w2[:], wts["w2"].rearrange("(c p) n -> p c n", p=P)).then_inc(weights_loaded, 16)
            sp.dma_start(state[:, 1:, :], x_v[1:NG].rearrange("g p d -> p g d")).then_inc(x_loaded, 16)
            with sp.Fori(1, NG) as g:
                sp.wait_ge(z_in_ready, g)
                sp.dma_start(ctx_in[:], ctx_v[g]).then_inc(ctx_loaded, 16)
            sp.wait_ge(empty_ready, 3)
            sp.dma_start(slots_v.rearrange("n p c -> p n c"),
                         empty_record[:].unsqueeze(1).to_broadcast([P, NS, REC])).then_inc(slots_emptied, 16)
            for n in range(8):
                sp.wait_ge(bank_filled[n], 2)
            sp.dma_start(e_w2[:], wts["e_w2"].rearrange("e f d -> (e f) d").rearrange("(k p) d -> p k d", p=P))\
              .then_inc(e_w2_loaded, 16)
            sp.dma_start(e_w1[:], wts["e_w1"].rearrange("e d f -> d e f")).then_inc(e_w1_loaded, 16)
            sp.wait_ge(slots_written, 16 * NT)
            for stage in (XB, LB):
                sp.wait_ge(bank_filled[stage.bank("out")], stage.count("out", NG - 1) + 1)
            for r in range(RING):
                sp.dma_start(slot_z[:, r, :], slots_v[r, :, 0:D]).then_inc(z_loaded[r], 16)
                sp.dma_start(slot_rest[:, r, :], slots_v[r, :, D:REC]).then_inc(rest_loaded[r], 16)
            with sp.Fori(1, NS // RING) as i:
                for r in range(RING):
                    bank = E.bank(("z", r))
                    sp.wait_ge(bank_filled[bank], E.count(("z", r), i - 1) + 1)
                    sp.dma_start(slot_z[:, r, :], slots_v[RING * i + r, :, 0:D]).then_inc(z_loaded[r], 16)
                    sp.wait_ge(rest_loaded[r], 16 * i)
                    sp.dma_start(slot_rest[:, RING * i + r, :], slots_v[RING * i + r, :, D:REC])\
                      .then_inc(rest_loaded[r], 16)
            for r in range(RING):
                sp.wait_ge(tokens_written[r], 16 * (NS // RING))

        @block.tensor
        def _(pe):
            mm = nc.tensor.matmul

            pe.wait_ge(consts_ready, 2)
            pe.wait_ge(raw_loaded, 16 * NRAW)
            for n in range(8):
                for m in range(4):
                    c = 4 * (n % 2) + m
                    last = nc.tensor.transpose(ps[n][:, m * P:(m + 1) * P],
                                               raw[RAW[n // 2]][:, c * P:(c + 1) * P], ident[:])
                last.then_inc(bank_filled[n], 1)
            for n in range(8):
                pe.wait_ge(bank_drained[n], 1)
            for n in range(8):
                par = slice((n % 2) * DH, (n % 2 + 1) * DH)
                if n < 4:
                    for m in range(4):
                        c = 4 * (n // 2) + m
                        last = mm(ps[n][:, m * P:(m + 1) * P], raw_t["Wq"][par, c, :],
                                  raw_t["Wk"][par, c, :], start=True, stop=True)
                else:
                    for c in range(8):
                        last = mm(ps[n][:, c * DH:(c + 1) * DH], raw_t[RAW[n // 2]][par, c, :],
                                  proj2[par, :], start=True, stop=True)
                last.then_inc(bank_filled[n], 1)
            pe.wait_ge(bank_drained[7], 2)
            nc.tensor.transpose(ps[7][:, 0:NE], gate_in[:], ident[0:NE, 0:NE])
            nc.tensor.transpose(ps[7][:, NE:NE + 4 * NE], b1_in[:], ident[0:4 * NE, 0:4 * NE])\
              .then_inc(bank_filled[7], 1)
            for n in range(8):
                pe.wait_ge(bank_drained[n], 3 if n == 7 else 2)
            pe.wait_ge(weights_loaded, 16 * NWTS)
            pe.wait_ge(wv_split, 2)

            def waits_alone():
                pe.sem_inc(pe_waits_passed, 1)

            def chunk(stage, name, g, reads=()):
                for bank, count in stage.needs(name, reads, g):
                    pe.wait_ge(bank_drained[bank], count)
                bank = stage.bank(name)
                return ps[bank], bank_filled[bank]

            def in_sbuf(stage, names, g):
                counts = {}
                for name in names:
                    counts[stage.bank(name)] = name
                for bank, name in counts.items():
                    pe.wait_ge(bank_drained[bank], stage.count(name, g) + 1)

            def turn_inputs(stage, name, g, z, ready=None):
                bank, filled = chunk(stage, name, g)
                if ready is not None:
                    pe.wait_ge(ready, g + 1)
                for n, rows in enumerate(z):
                    last = nc.tensor.transpose(bank[:, n * P:(n + 1) * P], rows, ident[:])
                last.then_inc(filled, 1)

            def split_product(bank, left, right):
                (left_hi, left_lo), (right_hi, right_lo) = left, right
                mm(bank[:], left_lo, right_hi, start=True, stop=False)
                mm(bank[:], left_hi, right_lo, start=False, stop=False)
                return mm(bank[:], left_hi, right_hi, start=False, stop=True)

            def x_latents(g):
                pe.wait_ge(z_in_ready, g + 1)
                turn_inputs(XF, "lat", g, [z_in[:, 0, :]])

            def x_context(g):
                turn_inputs(XF, "ctx", g, [z_in[:, 1 + b, :] for b in range(BG)])

            def x_t(g, k):
                bank, filled = chunk(XF, ("t", k), g, ["lat"] if k == 0 else [])
                for m in range(4):
                    last = mm(bank[:, m * P:(m + 1) * P], absorbed[:, 4 * k + m, :], lat_t[:],
                              start=True, stop=True)
                last.then_inc(filled, 1)

            def x_scores(g, b, c):
                bank, filled = chunk(XF, ("S", b, c), g, ["ctx", ("t", 2 * c), ("t", 2 * c + 1)])
                pe.wait_ge(ctx_split, g + 1)
                split_product(bank, [part[:, b * NC:(b + 1) * NC] for part in (ctx_hi, ctx_lo)],
                              [part[:, 8 * c:8 * c + 8, b * NL:(b + 1) * NL] for part in (t_hi, t_lo)])\
                    .then_inc(filled, 1)

            def x_values(g, b, c):
                bank, filled = chunk(XF, ("V", b, c), g)
                split_product(bank, [part[:, b * NC:(b + 1) * NC] for part in (ctx_hi, ctx_lo)],
                              [part[:, 0, c * 512:(c + 1) * 512] for part in (wv_hi, wv_lo)]).then_inc(filled, 1)

            def x_pv(g, q):
                bank, filled = chunk(XB, ("heads", q), g)
                if q == 0:
                    pe.wait_ge(probs_ready, g * (2 * BG) + 2 * BG)
                    in_sbuf(XF, [("V", 0, 0), ("V", 0, 1), ("V", 1, 0), ("V", 1, 1)], g)
                for b in range(BG):
                    for m in range(4):
                        h = 4 * q + m
                        last = mm(bank[b * NL:(b + 1) * NL, m * (DH + 1):(m + 1) * (DH + 1)],
                                  probs[:, b, h * NL:(h + 1) * NL], v_x[:, b, h, :],
                                  start=True, stop=True)
                last.then_inc(filled, 1)

            def turn(g, stage, o, c):
                bank, filled = chunk(stage, ("T", c), g, [("heads", 2 * c), ("heads", 2 * c + 1)])
                for m in range(4):
                    last = nc.tensor.transpose(bank[:, m * P:(m + 1) * P],
                                               o[:, (4 * c + m) * P:(4 * c + m + 1) * P], ident[:])
                last.then_inc(filled, 1)

            def out_projection(g, stage, ot, wo):
                bank, filled = chunk(stage, "out", g, [("T", 0), ("T", 1)])
                for c in range(8):
                    last = mm(bank[:, 0:D], ot[:, c * P:(c + 1) * P], wo[:, c, :],
                              start=(c == 0), stop=(c == 7))
                last.then_inc(filled, 1)

            def l_inputs(g):
                turn_inputs(LF, "h", g, [h_z[:]], h_z_ready)

            def l_qk(g, k):
                bank, filled = chunk(LF, ("qk", k), g, ["h"] if k == 0 else [])
                w = wq_phi if k < 2 else wk_phi
                for m in range(4):
                    c = 4 * (k % 2) + m
                    last = mm(bank[:, m * P:(m + 1) * P], w[:, c * P:(c + 1) * P], h_t[:],
                              start=True, stop=True)
                last.then_inc(filled, 1)

            def l_values(g, c):
                bank, filled = chunk(LF, ("v", c), g)
                pe.wait_ge(h_split, g + 1)
                split_product(bank, (h_hi[:], h_lo[:]),
                              [part[:, 1, c * 512:(c + 1) * 512] for part in (wv_hi, wv_lo)]).then_inc(filled, 1)

            def l_scores(g, par):
                rows = slice(par * DH, (par + 1) * DH)
                bank, filled = chunk(LF, ("A", par), g, [("qk", k) for k in range(4)])
                waits_alone()
                for b in range(BG):
                    tok = slice(b * NL, (b + 1) * NL)
                    for c in range(8):
                        last = mm(bank[tok, c * NL:(c + 1) * NL], k_t[rows, c, tok], q_t[rows, c, tok],
                                  start=True, stop=True)
                last.then_inc(filled, 1)

            def l_av(g, half):
                banks = [chunk(LB, ("heads", 2 * half + n), g) for n in range(2)]
                if half == 0:
                    in_sbuf(LF, [("A", 0), ("A", 1), ("v", 0), ("v", 1)], g)
                waits_alone()
                for b in range(BG):
                    rows = slice(b * NL, (b + 1) * NL)
                    for n, (bank, filled) in enumerate(banks):
                        for m in range(4):
                            h = 4 * (2 * half + n) + m
                            last = mm(bank[rows, m * (DH + 1):(m + 1) * (DH + 1)],
                                      a_t[rows, h % 2, h // 2, :], v_l[rows, h, :],
                                      start=True, stop=True)
                        if b == BG - 1:
                            last.then_inc(filled, 1)

            def f_inputs(g):
                turn_inputs(F, "h", g, [f_z[:]], f_z_ready)

            def f_up(g):
                bank, filled = chunk(F, "w1", g, ["h"])
                for c in range(4):
                    last = mm(bank[:, c * P:(c + 1) * P], w1[:, c * P:(c + 1) * P], f_t[:],
                              start=True, stop=True)
                last.then_inc(filled, 1)

            def f_down(g):
                bank, filled = chunk(F, "w2", g, ["w1"])
                for c in range(4):
                    last = mm(bank[:, 0:D], g_t[:, c, :], w2[:, c, :], start=(c == 0), stop=(c == 3))
                last.then_inc(filled, 1)

            def r_inputs(g):
                turn_inputs(F, "zr", g, [z_r[:]], z_r_ready)

            def r_gate(g):
                bank, filled = chunk(F, "gate", g, ["zr"])
                mm(bank[:, 0:NE], zr_t[:], gate_b1_t[:, 0:NE], start=True, stop=True).then_inc(filled, 1)

            def step(xf, xb, lf, lb, f, gi):
                on(lb, l_av, 0)
                on(xf, x_latents)
                on(f, f_inputs)
                on(lf, l_inputs)
                on(xb, x_pv, 0)
                on(xf, x_context)
                on(xf, x_t, 0)
                on(lf, l_qk, 0)
                on(xb, x_pv, 1)
                on(xf, x_t, 1)
                on(lf, l_qk, 1)
                on(lb, l_av, 1)
                on(xf, x_t, 2)
                on(lf, l_qk, 2)
                on(xb, x_pv, 2)
                on(xf, x_t, 3)
                on(lf, l_qk, 3)
                on(f, f_up)
                on(xb, x_pv, 3)
                on(lb, turn, LB, o_l, 0)
                on(xf, x_scores, 0, 0)
                on(lb, turn, LB, o_l, 1)
                on(xf, x_values, 0, 0)
                on(lf, l_scores, 0)
                on(xb, turn, XB, o_x, 0)
                on(lb, out_projection, LB, ot_l, wo_l)
                on(xf, x_values, 0, 1)
                on(xb, turn, XB, o_x, 1)
                on(xf, x_scores, 0, 1)
                on(f, f_down)
                on(lf, l_values, 0)
                on(xb, out_projection, XB, ot_x, wo_x)
                on(xf, x_scores, 1, 0)
                on(lf, l_scores, 1)
                on(xf, x_values, 1, 0)
                on(lf, l_values, 1)
                on(f, r_inputs)
                on(xf, x_scores, 1, 1)
                on(xf, x_values, 1, 1)
                on(f, r_gate)

            steps(pe, step)

            pe.wait_ge(chosen_ready, 1)
            bank, filled = chunk(R, "rank", 0)
            flat = chosen[:].rearrange("p t e -> p (t e)")
            mm(bank[:, 0:NT * NE], earlier_row[:], flat, start=True, stop=True)
            mm(bank[:, NT * NE:2 * NT * NE], ones[:], flat, start=True, stop=True).then_inc(filled, 1)

            def e_z(i, r):
                pe.wait_ge(z_loaded[r], 16 * i + 16)
                bank, filled = chunk(E, ("z", r), i)
                nc.tensor.transpose(bank[:, 0:P], slot_z[:, r, :], ident[:]).then_inc(filled, 1)

            def e_up(i, r):
                pe.wait_ge(w1_now_ready, RING * i + (r + 1))
                for n, name in enumerate(("hA", "hB")):
                    bank, filled = chunk(E, (name, r), i, [("z", r)])
                    for m in range(2):
                        c = 2 * n + m
                        last = mm(bank[:, m * P:(m + 1) * P], w1_now[:, r % 2, c * P:(c + 1) * P],
                                  slot_t[:, r % 2, :], start=True, stop=True)
                    last.then_inc(filled, 1)

            def e_down(i, r, expert):
                bank, filled = chunk(E, ("y", r), i, [("hA", r), ("hB", r)])
                for c in range(4):
                    last = mm(bank[:, 0:D], hid_t[:, r % 2, c, :], e_w2[:, expert * 4 + c, :],
                              start=(c == 0), stop=(c == 3))
                last.then_inc(filled, 1)

            def tiles(i, first, last):
                expert = experts_near(pe, i)
                if first:
                    e_z(i, 0)
                for r in range(RING):
                    if r + 1 < RING:
                        e_z(i, r + 1)
                    elif not last:
                        e_z(i + 1, 0)
                    e_up(i, r)
                    if r > 0:
                        e_down(i, r - 1, expert(r - 1))
                    elif not first:
                        e_down(i - 1, RING - 1, expert(-1))
                if last:
                    e_down(i, RING - 1, expert(RING - 1))

            pe.wait_ge(experts_known, 1)
            pe.wait_ge(e_w2_loaded, 16)
            tile_steps(pe, tiles)

        @block.scalar
        def _(act):
            for n, name in enumerate(["ln_l_w", "ln_l_b", "ln_c_w", "ln_c_b", "g1", "beta1", "g2", "beta2"]):
                act.dma_start(cols[:, n:n + 1], wts[name].rearrange("(p a) -> p a", a=1)).then_inc(cols_loaded, 16)
            for c in range(4):
                act.dma_start(cols[:, 8 + c:9 + c], wts["b1"][c * P:(c + 1) * P].rearrange("(p a) -> p a", a=1))\
                   .then_inc(cols_loaded, 16)
            for n in range(0, 8, 2):
                act.wait_ge(bank_filled[n], 1)
                nc.scalar.activation(raw_t[RAW[n // 2]][:, 0:4, :], ps[n][:].rearrange("p (c m) -> p c m", m=P),
                                     ACT.Copy).then_inc(bank_drained[n], 1)
            for n in range(0, 8, 2):
                act.wait_ge(bank_filled[n], 2)
                if n < 4:
                    dst = absorbed[:, 8 * (n // 2):8 * (n // 2) + 8:2, :]
                    src = ps[n][:].rearrange("p (c m) -> p c m", m=P)
                else:
                    dst = (wq_phi if n == 4 else wk_phi)[:].rearrange("p (c h e) -> p c h e", h=2, e=DH)[:, :, 0, :]
                    src = ps[n][:].rearrange("p (c e) -> p c e", e=DH)
                nc.scalar.activation(dst, src, ACT.Copy).then_inc(bank_drained[n], 1)
            act.wait_ge(cols_loaded, 16 * NCOLS)

            def filled(stage, name, g):
                bank = stage.bank(name)
                act.wait_ge(bank_filled[bank], stage.count(name, g) + 1)
                return ps[bank], bank_drained[bank]

            def taken(stage, name, g):
                act.wait_ge(bank_drained[stage.bank(name)], stage.count(name, g) + 1)

            def copy_out(stage, name, g, dst, src=lambda bank: bank[:]):
                bank, drained = filled(stage, name, g)
                nc.scalar.activation(dst, src(bank), ACT.Copy).then_inc(drained, 1)

            def x_context(g):
                bank, drained = filled(XF, "ctx", g)
                for dst in (ctx_t, ctx_hi):
                    last = nc.scalar.activation(dst[:], bank[:, 0:BG * NC], ACT.Identity, scale=cols[:, 2:3],
                                                bias=cols[:, 3:4])
                last.then_inc(drained, 1)

            def x_t(g, k):
                bank, _ = filled(XF, ("t", k), g)
                nc.scalar.activation(t_hi[:, 4 * k:4 * k + 4, :], bank[:].rearrange("p (m t) -> p m t", m=4),
                                     ACT.Copy).then_inc(t_hi_ready, 1)

            def by_head(bank):
                return bank[:].rearrange("p (h e) -> p h e", e=DH)

            def x_values(g, b, c):
                copy_out(XF, ("V", b, c), g, v_x[:, b, 8 * c:8 * c + 8, 0:DH], by_head)

            def l_values(g, c):
                copy_out(LF, ("v", c), g, v_l[:, 8 * c:8 * c + 8, 0:DH], by_head)

            def turned(g, stage, ot, c):
                copy_out(stage, ("T", c), g, ot[:, c * 512:(c + 1) * 512])

            def x_exp(g, b, c):
                n = 2 * b + c
                taken(XF, ("S", b, c), g)
                nc.scalar.activation(probs[:, b, c * 512:(c + 1) * 512], clipped[:, n % 2, :], ACT.Exp,
                                     scale=SCALE).then_inc(probs_ready, 1)

            def l_exp(g, k):
                bank, _ = filled(LF, ("qk", k), g)
                nc.scalar.activation(neg_relu[:, k % 2, :], bank[:], ACT.Relu, scale=-1.0).then_inc(relu_ready, 1)
                act.wait_ge(relu_ready, g * 4 + (k + 1))
                if k >= 2:
                    taken(LF, ("qk", k - 2), g)
                nc.scalar.activation(phi_exp[:, k % 2, :], neg_relu[:, k % 2, :], ACT.Exp,
                                     scale=-1.0).then_inc(phi_exp_ready, 1)

            def f_gelu(g):
                bank, drained = filled(F, "w1", g)
                for c in range(4):
                    last = nc.scalar.activation(g_t[:, c, :], bank[:, c * P:(c + 1) * P], ACT.Gelu,
                                                bias=cols[:, 8 + c:9 + c])
                last.then_inc(drained, 1)
                nc.scalar.activation(exp_of_zero[:], zero[:], ACT.Exp).then_inc(table_in, 1)
                act.wait_ge(table_in, g + 1)

            def step(xf, xb, lf, lb, f, gi):
                on(xf, x_context)
                for k in range(4):
                    on(xf, x_t, k)
                    on(lf, l_exp, k)
                on(lb, turned, LB, ot_l, 0)
                on(lb, turned, LB, ot_l, 1)
                on(xf, x_exp, 0, 0)
                on(xf, x_values, 0, 0)
                on(xb, turned, XB, ot_x, 0)
                on(f, f_gelu)
                on(xb, turned, XB, ot_x, 1)
                on(xf, x_values, 0, 1)
                on(xf, x_exp, 0, 1)
                on(lf, l_values, 0)
                on(xf, x_exp, 1, 0)
                on(xf, x_values, 1, 0)
                on(lf, l_values, 1)
                on(xf, x_exp, 1, 1)
                on(xf, x_values, 1, 1)

            steps(act, step)

            def e_relu(i, r, expert):
                bank, drained = filled(E, ("hA", r), i)
                for c in range(2):
                    last = nc.scalar.activation(hid_t[:, r % 2, c, :], bank[:, c * P:(c + 1) * P], ACT.Relu,
                                                bias=gate_b1_t[:, bass.ds(expert * 4 + (NE + c), 1)])
                last.then_inc(drained, 1)

            def e_first(i, r, expert):
                if not (isinstance(i, int) and i == 0 and r < 2):
                    bank = E.bank(("z", r))
                    act.wait_ge(bank_filled[bank], E.count(("z", r), i) + 1)
                nc.scalar.activation(w1_now[:, r % 2, :], e_w1[:, expert, :], ACT.Copy).then_inc(w1_now_ready, 1)

            def tiles(i, first, last):
                expert = experts_near(act, i)
                if first:
                    e_first(i, 0, expert(0))
                for r in range(RING):
                    if r + 1 < RING:
                        e_first(i, r + 1, expert(r + 1))
                    elif not last:
                        e_first(i + 1, 0, expert(RING))
                    e_relu(i, r, expert(r))

            act.wait_ge(experts_known, 1)
            act.wait_ge(e_w1_loaded, 16)
            tile_steps(act, tiles)

        @block.vector
        def _(dve):
            V = nc.vector
            V.memset(v_x[:, :, :, DH:DH + 1], 1.0)
            V.memset(v_l[:, :, DH:DH + 1], 1.0)
            V.memset(per_tile[:], 0.0)
            V.memset(zero[:], 0.0)
            V.memset(minus_half[:], -0.5).then_inc(consts_ready, 1)

            def waits_alone():
                dve.sem_inc(dve_waits_passed, 1)

            class Own:

                def __init__(self, landed, per_pair):
                    self.landed, self.per_pair, self.n = landed, per_pair, 0

                def land(self, g, instruction):
                    self.n += 1
                    instruction.then_inc(self.landed, 1)
                    dve.wait_ge(self.landed, g * self.per_pair + self.n)
                    self.n %= self.per_pair

            of_in, of_x, of_l, of_f = Own(in_step, 2), Own(x_step, 6), Own(l_step, 10), Own(f_step, 3)

            def filled(stage, name, g):
                bank = stage.bank(name)
                dve.wait_ge(bank_filled[bank], stage.count(name, g) + 1)
                return ps[bank], bank_drained[bank]

            def taken(stage, name, g):
                dve.wait_ge(bank_drained[stage.bank(name)], stage.count(name, g) + 1)

            def var_once(dst, var):
                return V.tensor_scalar(dst, var, EPS, None, ALU.add)

            def var_twice(dst, var):
                return V.tensor_scalar(dst, var, 1.0 + EPS, EPS * EPS, ALU.mult, ALU.add)

            def normalise(dst, src, mv, rstd):
                return V.tensor_scalar(dst, src, mv[:, 0:1], rstd, ALU.subtract, ALU.mult)

            def in_stats(g):
                if isinstance(g, int) and g == 0:
                    dve.wait_ge(x_first_loaded, 16)
                else:
                    dve.wait_ge(x_loaded, 16)
                dve.wait_ge(ctx_loaded, 16 * g + 16)
                waits_alone()
                V.bn_stats(st_in[:, 0, :], state[:, g, :])
                for b in range(BG):
                    last = V.bn_stats(st_in[:, 1 + b, :], ctx_in[:, b, :])
                of_in.land(g, last)
                waits_alone()
                for n in range(1 + BG):
                    last = V.bn_aggr(mv_in[:, n, :], st_in[:, n, :])
                of_in.land(g, last)
                var_twice(var_in[:, 0:1], mv_in[:, 0:1, 1])
                var_once(var_in[:, 1:], mv_in[:, 1:, 1]).then_inc(var_in_ready, 1)

            def in_normalise(g):
                if not (isinstance(g, int) and g == 0):
                    dve.wait_ge(bank_filled[XF.bank("ctx")], XF.count("ctx", g - 1) + 1)
                dve.wait_ge(rstd_in_ready, g + 1)
                normalise(z_in[:, 0, :], state[:, g, :], mv_in[:, 0, :], rstd_in[:, 0:1])
                for b in range(BG):
                    last = normalise(z_in[:, 1 + b, :], ctx_in[:, b, :], mv_in[:, 1 + b, :],
                                     rstd_in[:, 1 + b:2 + b])
                last.then_inc(z_in_ready, 1)

            def affine_out(g, stage, name, dst, col):
                bank, drained = filled(stage, name, g)
                V.tensor_scalar(dst[:], bank[:, 0:P], cols[:, col:col + 1], cols[:, col + 1:col + 2],
                                ALU.mult, ALU.add).then_inc(drained, 1)

            def x_t_low(g, k):
                bank, drained = filled(XF, ("t", k), g)
                dve.wait_ge(t_hi_ready, g * 4 + (k + 1))
                V.tensor_tensor(t_lo[:, 4 * k:4 * k + 4, :], bank[:].rearrange("p (m t) -> p m t", m=4),
                                t_hi[:, 4 * k:4 * k + 4, :].bitcast(F32), ALU.subtract).then_inc(drained, 1)

            def l_phi(g, k):
                bank, drained = filled(LF, ("qk", k), g)
                dve.wait_ge(phi_exp_ready, g * 4 + (k + 1))
                V.scalar_tensor_tensor(out=qk_t[:, 4 * k:4 * k + 4, :].rearrange("p a b -> p (a b)"),
                                       in0=bank[:], scalar=0.0, in1=phi_exp[:, k % 2, :],
                                       op0=ALU.max, op1=ALU.add).then_inc(drained, 1)

            def x_clip(g, b, c):
                n = 2 * b + c
                if n >= 2:
                    dve.wait_ge(probs_ready, g * (2 * BG) + (n - 1))
                bank, drained = filled(XF, ("S", b, c), g)
                V.tensor_scalar(clipped[:, n % 2, :], bank[:], -CLIP / SCALE, CLIP / SCALE,
                                ALU.max, ALU.min).then_inc(drained, 1)

            def l_mask(g, par):
                bank, drained = filled(LF, ("A", par), g)
                V.tensor_tensor(a_t[:, par, :, :], bank[:].rearrange("p (c t) -> p c t", t=NL),
                                causal[:].unsqueeze(1).to_broadcast([P, 8, NL]), ALU.mult).then_inc(drained, 1)

            def divide_heads(g, stage, q, dst, own, eps=None):
                bank, drained = filled(stage, ("heads", q), g)
                heads = bank[:, 0:4 * (DH + 1)].rearrange("p (h e) -> p h e", e=DH + 1)
                r = (rden_l if eps else rden_x)[:, q % 2, :]
                if eps:
                    d = den_l[:, q % 2, :]
                    own.land(g, V.tensor_scalar(d, heads[:, :, DH], eps, None, ALU.add))
                    own.land(g, V.reciprocal(r, d))
                else:
                    own.land(g, V.reciprocal(r, heads[:, :, DH]))
                V.tensor_tensor(dst[:, q * 256:(q + 1) * 256].rearrange("p (h e) -> p h e", e=DH),
                                heads[:, :, 0:DH], r.unsqueeze(2).to_broadcast([P, 4, DH]),
                                ALU.mult).then_inc(drained, 1)

            def row_stats(g, src, st, mv, own):
                waits_alone()
                own.land(g, V.bn_stats(st[:], src))
                waits_alone()
                own.land(g, V.bn_aggr(mv[:], st[:]))

            def l_finish(g):
                bank, drained = filled(LB, "out", g)
                if not (isinstance(g, int) and g == 0):
                    dve.wait_ge(b2_added, g)
                V.tensor_tensor(zf[:], bank[:, 0:D], records[:, g, 0:D], ALU.add).then_inc(drained, 1)
                taken(LB, "out", g)
                row_stats(g, zf[:], st_z, mv_z, of_l)
                var_once(var_z[:], mv_z[:, 1:2]).then_inc(var_z_ready, 1)

            def l_normalise(g):
                dve.wait_ge(rstd_z_ready, g + 1)
                normalise(f_z[:], zf[:], mv_z, rstd_z[:, 0:1]).then_inc(f_z_ready, 1)

            def x_finish(g):
                bank, drained = filled(XB, "out", g)
                dve.wait_ge(bo_added, g + 1)
                V.tensor_tensor(state[:, g, :], bank[:, 0:D], x_plus_bo[:], ALU.add).then_inc(drained, 1)
                taken(XB, "out", g)
                row_stats(g, state[:, g, :], st_x1, mv_x1, of_x)
                var_once(var_x1[:, 0:1], mv_x1[:, 1:2])
                var_twice(var_x1[:, 1:2], mv_x1[:, 1:2]).then_inc(var_x1_ready, 1)

            def x_normalise(g):
                dve.wait_ge(rstd_x1_ready, g + 1)
                normalise(records[:, g, 0:D], state[:, g, :], mv_x1, rstd_x1[:, 0:1])
                normalise(h_z[:], state[:, g, :], mv_x1, rstd_x1[:, 1:2]).then_inc(h_z_ready, 1)

            def f_finish(g):
                bank, drained = filled(F, "w2", g)
                dve.wait_ge(b2_added, g + 1)
                V.tensor_tensor(f_sum[:], bank[:, 0:D], zf_b2[:], ALU.add).then_inc(drained, 1)
                taken(F, "w2", g)
                of_f.land(g, V.tensor_tensor(records[:, g, D:2 * D], state[:, g, :], f_sum[:], ALU.add))
                row_stats(g, records[:, g, D:2 * D], st_r, mv_r, of_f)
                var_once(var_r[:], mv_r[:, 1:2]).then_inc(var_r_ready, 1)

            def r_normalise(g):
                dve.wait_ge(rstd_r_ready, g + 1)
                normalise(records[:, g, 0:D], records[:, g, D:2 * D], mv_r, rstd_r[:, 0:1])
                normalise(z_r[:], records[:, g, D:2 * D], mv_r, rstd_r[:, 0:1]).then_inc(z_r_ready, 1)

            def r_turned(g):
                bank, drained = filled(F, "zr", g)
                V.tensor_copy(zr_t[:], bank[:, 0:P]).then_inc(drained, 1)

            def r_logits(g):
                bank, drained = filled(F, "gate", g)
                V.tensor_tensor(logits[:, g, :], bank[:, 0:NE], gate_b_row[:], ALU.add).then_inc(drained, 1)

            def step(xf, xb, lf, lb, f, gi):
                on(xf, affine_out, XF, "lat", lat_t, 0)
                on(lf, affine_out, LF, "h", h_t, 4)
                on(lb, divide_heads, LB, 0, o_l, of_l, 1e-6)
                on(xb, divide_heads, XB, 0, o_x, of_x)
                on(lb, divide_heads, LB, 1, o_l, of_l, 1e-6)
                on(xf, x_t_low, 0)
                on(f, affine_out, F, "h", f_t, 6)
                on(xb, divide_heads, XB, 1, o_x, of_x)
                on(lf, l_phi, 0)
                on(xf, x_t_low, 1)
                on(lf, l_phi, 1)
                on(lb, divide_heads, LB, 2, o_l, of_l, 1e-6)
                on(xf, x_t_low, 2)
                on(lb, divide_heads, LB, 3, o_l, of_l, 1e-6)
                on(lf, l_phi, 2)
                on(xb, divide_heads, XB, 2, o_x, of_x)
                on(xf, x_t_low, 3)
                on(lf, l_phi, 3)
                on(xf, x_clip, 0, 0)
                on(xb, divide_heads, XB, 3, o_x, of_x)
                on(lf, l_mask, 0)
                on(gi, in_stats)
                on(lb, l_finish)
                on(xf, x_clip, 0, 1)
                on(lb, l_normalise)
                on(f, f_finish)
                on(xb, x_finish)
                on(f, r_normalise)
                on(xf, x_clip, 1, 0)
                on(lf, l_mask, 1)
                on(xb, x_normalise)
                on(f, r_turned)
                on(gi, in_normalise)
                on(xf, x_clip, 1, 1)
                on(f, r_logits)

            in_stats(0)
            for n in range(1, 8, 2):
                dve.wait_ge(bank_filled[n], 1)
                V.tensor_copy(raw_t[RAW[n // 2]][:, 4:8, :],
                              ps[n][:].rearrange("p (c m) -> p c m", m=P)).then_inc(bank_drained[n], 1)
            in_normalise(0)
            for n in range(1, 8, 2):
                dve.wait_ge(bank_filled[n], 2)
                if n < 4:
                    dst = absorbed[:, 8 * (n // 2) + 1:8 * (n // 2) + 8:2, :]
                    src = ps[n][:].rearrange("p (c m) -> p c m", m=P)
                else:
                    dst = (wq_phi if n == 5 else wk_phi)[:].rearrange("p (c h e) -> p c h e", h=2, e=DH)[:, :, 1, :]
                    src = ps[n][:].rearrange("p (c e) -> p c e", e=DH)
                V.tensor_copy(dst, src).then_inc(bank_drained[n], 1)
            dve.wait_ge(bank_filled[7], 3)
            V.tensor_copy(gate_b1_t[:], ps[7][:, 0:5 * NE]).then_inc(bank_drained[7], 1)
            dve.wait_ge(cols_loaded, 16 * NCOLS)
            dve.wait_ge(consts_ready, 2)
            dve.wait_ge(rows_loaded, 16 * NROWS)
            dve.wait_ge(weights_loaded, 16 * NWTS)
            V.tensor_copy(wv_hi[:], wv_raw[:]).then_inc(wv_split, 1)
            dve.wait_ge(wv_split, 1)
            V.tensor_tensor(wv_lo[:], wv_raw[:], wv_hi[:].bitcast(F32), ALU.subtract).then_inc(wv_split, 1)
            steps(dve, step)

            of_route = Own(route_step, 1 << 30)

            def now(instruction):
                of_route.land(0, instruction)

            def by_tile(tile):
                return tile[:].rearrange("p (t e) -> p t e", e=NE)

            def over_tiles(row):
                return row.unsqueeze(1).to_broadcast([P, NT, NE])

            w = [by_tile(t) for t in work]
            taken(F, "gate", NG - 1)
            now(V.tensor_tensor(logits[:], logits[:], over_tiles(expert_bias_row[:]), ALU.add))
            now(V.tensor_reduce(best[:, 0, :], logits[:], AX.X, ALU.max))
            now(V.tensor_tensor(w[0], logits[:], best[:, 0, :].unsqueeze(2).to_broadcast([P, NT, NE]), ALU.is_ge))
            now(V.scalar_tensor_tensor(out=w[1], in0=w[0], scalar=-float(NE), in1=over_tiles(iota_e[:]),
                                       op0=ALU.mult, op1=ALU.add))
            now(V.tensor_reduce(best[:, 1, :], w[1], AX.X, ALU.min))
            V.tensor_tensor(chosen[:], over_tiles(expert_m8[:]), best[:, 1, :].unsqueeze(2).to_broadcast([P, NT, NE]),
                            ALU.is_equal).then_inc(chosen_ready, 1)
            bank, drained = filled(R, "rank", 0)
            totals = bank[:, NT * NE:2 * NT * NE].rearrange("p (t e) -> p t e", e=NE)
            now(V.tensor_copy(w[0], totals))
            a, b, reach = w[0], w[1], 1
            while reach < NT:
                V.tensor_copy(b[:, 0:reach, :], a[:, 0:reach, :])
                now(V.tensor_tensor(b[:, reach:, :], a[:, reach:, :], a[:, 0:NT - reach, :], ALU.add))
                a, b, reach = b, (w[2] if b is w[1] else w[1]), 2 * reach
            counts = a[:, NT - 1, :]
            now(V.tensor_tensor(w[3].rearrange("p t e -> p e t"), counts.unsqueeze(2).to_broadcast([P, NE, NT]),
                                thresholds[:].unsqueeze(1).to_broadcast([P, NE, NT]), ALU.is_gt))
            now(V.tensor_reduce(tiles_of[:, 0, :], w[3].rearrange("p t e -> p e t"), AX.X, ALU.add))
            now(V.tensor_tensor(earlier_expert[:], earlier_expert[:],
                                tiles_of[:, 0, :].unsqueeze(1).to_broadcast([P, NE, NE]), ALU.mult))
            now(V.tensor_reduce(tiles_of[:, 1, :], earlier_expert[:], AX.X, ALU.add))
            now(V.tensor_tensor(tiles_of[:, 2, :], tiles_of[:, 0, :], tiles_of[:, 1, :], ALU.add))
            now(V.tensor_tensor(a, a, w[0], ALU.subtract))
            V.tensor_tensor(b, bank[:, 0:NT * NE].rearrange("p (t e) -> p t e", e=NE), a, ALU.add).then_inc(drained, 1)
            taken(R, "rank", 0)
            now(V.scalar_tensor_tensor(out=w[3], in0=over_tiles(tiles_of[:, 1, :]), scalar=float(P), in1=b,
                                       op0=ALU.mult, op1=ALU.add))
            now(V.tensor_tensor(w[3], w[3], chosen[:], ALU.mult))
            now(V.tensor_reduce(best[:, 0, :], w[3], AX.X, ALU.add))
            V.tensor_copy(slot_of[:], best[:, 0, :]).then_inc(slots_known, 1)
            ends = tile_ends[0:1, :, :]
            now(V.tensor_tensor(ends, tiles_of[0:1, 2, :].unsqueeze(1).to_broadcast([1, NS, NE]),
                                tile_no[0:1, :].unsqueeze(2).to_broadcast([1, NS, NE]), ALU.is_le))
            now(V.tensor_reduce(per_tile[0:1, 1:1 + NS], ends, AX.X, ALU.add))
            now(V.tensor_scalar(per_tile[0:1, 1:1 + NS], per_tile[0:1, 1:1 + NS], float(NE - 1), None, ALU.min))
            column = [per_tile[0:1, m:m + NS - RING + 1:RING] for m in range(RING + 2)]
            now(V.tensor_copy(packed[:, 0, :], column[RING + 1]))
            for m in range(RING, 0, -1):
                now(V.scalar_tensor_tensor(out=packed[:, (RING + 1 - m) % 2, :], in0=packed[:, (RING - m) % 2, :],
                                           scalar=float(NE), in1=column[m], op0=ALU.mult, op1=ALU.add))
            V.scalar_tensor_tensor(out=experts_of[:], in0=packed[:, RING % 2, :], scalar=float(NE), in1=column[0],
                                   op0=ALU.mult, op1=ALU.add).then_inc(experts_known, 1)

            def e_inputs(i, r):
                bank, drained = filled(E, ("z", r), i)
                V.tensor_copy(slot_t[:, r % 2, :], bank[:, 0:P]).then_inc(drained, 1)

            def e_relu(i, r, expert):
                bank, drained = filled(E, ("hB", r), i)
                for m in range(2):
                    b1 = gate_b1_t[:, bass.ds(expert * 4 + (NE + 2 + m), 1)]
                    last = V.tensor_scalar(hid_t[:, r % 2, 2 + m, :], bank[:, m * P:(m + 1) * P], b1, 0.0,
                                           ALU.add, ALU.max)
                last.then_inc(drained, 1)

            def e_finish(i, r, expert):
                dve.wait_ge(rest_loaded[r], 16 * i + 16)
                if not (isinstance(i, int) and i == 0):
                    dve.wait_ge(tokens_written[r], 16 * i)
                V.tensor_copy(token_no[:, r:r + 1], slot_rest[:, RING * i + r, D:].bitcast(U32))
                V.tensor_tensor(x2_b2[:, r % 2, :], slot_rest[:, RING * i + r, 0:D], e_b2[:, bass.ds(expert * D, D)],
                                ALU.add).then_inc(b2_ready, 1)
                dve.wait_ge(b2_ready, RING * i + (r + 1))
                bank, drained = filled(E, ("y", r), i)
                V.tensor_tensor(slot_out[:, r, :], bank[:, 0:D], x2_b2[:, r % 2, :], ALU.add).then_inc(drained, 1)

            def tiles(i, first, last):
                expert = experts_near(dve, i)
                if first:
                    e_inputs(i, 0)
                for r in range(RING):
                    if r + 1 < RING:
                        e_inputs(i, r + 1)
                    elif not last:
                        e_inputs(i + 1, 0)
                    e_relu(i, r, expert(r))
                    if r > 0:
                        e_finish(i, r - 1, expert(r - 1))
                    elif not first:
                        e_finish(i - 1, RING - 1, expert(-1))
                if last:
                    e_finish(i, RING - 1, expert(RING - 1))

            dve.wait_ge(experts_known, 1)
            tile_steps(dve, tiles)

        @block.gpsimd
        def _(pool):
            G = nc.gpsimd
            G.memset(ident[:], 0.0).then_inc(ident_zeroed, 1)
            G.memset(causal[:], 1.0).then_inc(ident_zeroed, 1)
            pool.dma_start(bo_row[:], wts["bo"].partition_broadcast(P)).then_inc(rows_loaded, 16)
            pool.dma_start(b2_row[:], wts["b2"].partition_broadcast(P)).then_inc(rows_loaded, 16)
            pool.dma_start(gate_b_row[:], wts["gate_b"].partition_broadcast(P)).then_inc(rows_loaded, 16)
            pool.dma_start(expert_bias_row[:], wts["expert_bias"].partition_broadcast(P)).then_inc(rows_loaded, 16)
            pool.dma_start(e_b2[:], wts["e_b2"].rearrange("e d -> (e d)").partition_broadcast(P)).then_inc(rows_loaded, 16)
            pool.wait_ge(ident_zeroed, 2)
            for half in range(2):
                part = causal[half * NL:(half + 1) * NL, :]
                G.affine_select(out=part, in_=part, compare_op=ALU.is_ge, fill=0.0, base=0,
                                pattern=[[1, NL]], channel_multiplier=-1).then_inc(causal_half, 1)
                pool.wait_ge(causal_half, half + 1)
            G.affine_select(out=ident[:], in_=ident[:], compare_op=ALU.not_equal, fill=1.0, base=0,
                            pattern=[[-1, P]], channel_multiplier=1).then_inc(consts_ready, 1)
            G.memset(empty_record[:], 0.0).then_inc(empty_ready, 1)
            pool.wait_ge(empty_ready, 1)
            G.iota(empty_record[:, 2 * D:REC].bitcast(U32), pattern=[[0, 1]], base=NOBODY,
                   channel_multiplier=0).then_inc(empty_ready, 1)
            pool.wait_ge(empty_ready, 2)
            G.iota(records[:, :, 2 * D:REC].bitcast(U32), pattern=[[P, NT], [0, 1]], base=0, channel_multiplier=1)
            for tile, start, stride in ((expert_m8, -NE, 1), (iota_e, 0, 1), (thresholds, 0, P), (tile_no, 0, 1)):
                G.iota(tile[:], pattern=[[stride, tile.shape[1]]], base=start, channel_multiplier=0,
                       allow_small_or_imprecise_dtypes=True)
            G.memset(ones[:], 1.0)
            G.memset(earlier_row[:], 1.0)
            G.memset(earlier_expert[:], 1.0).then_inc(empty_ready, 1)
            pool.wait_ge(empty_ready, 3)
            G.affine_select(out=earlier_row[:], in_=earlier_row[:], compare_op=ALU.is_ge, fill=0.0, base=-1,
                            pattern=[[1, P]], channel_multiplier=-1)
            G.affine_select(out=earlier_expert[:], in_=earlier_expert[:], compare_op=ALU.is_ge, fill=0.0, base=-1,
                            pattern=[[1, NE], [-1, NE]], channel_multiplier=0).then_inc(routing_consts, 1)
            pool.wait_ge(routing_consts, 1)
            pool.wait_ge(consts_ready, 2)
            pool.wait_ge(rows_loaded, 16 * NROWS)

            def power(var, rstd, ready, powered, g, n):
                pool.wait_ge(ready, g + 1)
                G.tensor_tensor(rstd, var, minus_half[:, 0:n], ALU.pow).then_inc(powered, 1)

            def taken(stage, name, g):
                pool.wait_ge(bank_drained[stage.bank(name)], stage.count(name, g) + 1)

            def add_bo(g):
                if isinstance(g, int) and g == 0:
                    pool.wait_ge(x_first_loaded, 16)
                else:
                    pool.wait_ge(x_loaded, 16)
                    taken(XB, "out", g - 1)
                G.tensor_tensor(x_plus_bo[:], state[:, g, :], bo_row[:], ALU.add).then_inc(bo_added, 1)

            def x_context_low(g):
                taken(XF, "ctx", g)
                G.tensor_tensor(ctx_lo[:], ctx_t[:], ctx_hi[:].bitcast(F32), ALU.subtract).then_inc(ctx_split, 1)

            def l_split(g):
                taken(LF, "h", g)
                pool.sem_inc(pool_waits_passed, 1)
                G.tensor_copy(h_hi[:], h_t[:]).then_inc(h_hi_ready, 1)
                pool.wait_ge(h_hi_ready, g + 1)
                G.tensor_tensor(h_lo[:], h_t[:], h_hi[:].bitcast(F32), ALU.subtract).then_inc(h_split, 1)

            def add_b2(g):
                taken(LB, "out", g)
                if not (isinstance(g, int) and g == 0):
                    taken(F, "w2", g - 1)
                G.tensor_tensor(zf_b2[:], zf[:], b2_row[:], ALU.add).then_inc(b2_added, 1)

            def rstd_of_in(g):
                power(var_in[:], rstd_in[:], var_in_ready, rstd_in_ready, g, 1 + BG)

            def rstd_of_r(g):
                power(var_r[:], rstd_r[:], var_r_ready, rstd_r_ready, g, 1)

            def rstd_of_z(g):
                power(var_z[:], rstd_z[:], var_z_ready, rstd_z_ready, g, 1)

            def rstd_of_x1(g):
                power(var_x1[:], rstd_x1[:], var_x1_ready, rstd_x1_ready, g, 2)

            def step(xf, xb, lf, lb, f, gi):
                on(xb, add_bo)
                on(xf, x_context_low)
                on(lf, l_split)
                on(gi, rstd_of_in)
                on(lb, rstd_of_z)
                on(f, rstd_of_r)
                on(lb, add_b2)
                on(xb, rstd_of_x1)

            rstd_of_in(0)
            steps(pool, step)

            pool.wait_ge(slots_emptied, 16)
            pool.wait_ge(slots_known, 1)
            pool.wait_ge(z_r_ready, NG)
            for t in range(NT):
                pool.indirect_dma_start(slots, bass.IndirectOffsetOnAxis(ap=slot_of[:, t:t + 1], axis=0),
                                        records[:, t, :], None).then_inc(slots_written, 16)

            def tiles(i, first, last):
                for r in range(RING):
                    pool.wait_ge(bank_drained[E.bank(("y", r))], E.count(("y", r), i) + 1)
                    pool.sem_inc(pool_waits_passed, 1)
                    pool.indirect_dma_start(
                        out_rows, bass.IndirectOffsetOnAxis(ap=token_no[:, r:r + 1], axis=0),
                        slot_out[:, r, :], None, bounds_check=NB * NL - 1, oob_is_err=False)\
                        .then_inc(tokens_written[r], 16)

            tile_steps(pool, tiles)


_WEIGHTS = {
    "ln_l_w": "L0_xattn_ln_l_w", "ln_l_b": "L0_xattn_ln_l_b", "ln_c_w": "L0_xattn_ln_c_w",
    "ln_c_b": "L0_xattn_ln_c_b", "Wq": "L0_xattn_Wq", "Wkv": "L0_xattn_Wkv", "Wo": "L0_xattn_Wo",
    "bo": "L0_xattn_bo", "wq": "L0_attn_wq", "wk": "L0_attn_wk", "wv": "L0_attn_wv", "wo": "L0_attn_wo",
    "proj": "L0_attn_proj", "w1": "L0_attn_w1", "b1": "L0_attn_b1", "w2": "L0_attn_w2", "b2": "L0_attn_b2",
    "g1": "L0_attn_g1", "beta1": "L0_attn_beta1", "g2": "L0_attn_g2", "beta2": "L0_attn_beta2",
    "gate_w": "L0_ffn_gate_w", "gate_b": "L0_ffn_gate_b", "expert_bias": "L0_ffn_expert_bias",
    "e_w1": "L0_ffn_w1", "e_b1": "L0_ffn_b1", "e_w2": "L0_ffn_w2", "e_b2": "L0_ffn_b2",
}


def kernel(**inputs):
    import numpy as _np
    import concourse.bacc as _bacc
    from concourse import mybir as _mybir
    from concourse.bass_utils import run_bass_kernel_spmd as _run

    nc = _bacc.Bacc("TRN2", target_bir_lowering=False, num_devices=1)
    arrays = {}

    def dram(name):
        a = _np.ascontiguousarray(inputs[name])
        arrays[f"in_{name}_dram"] = a
        return nc.dram_tensor(f"in_{name}_dram", a.shape, _mybir.dt.from_np(a.dtype), kind="ExternalInput").ap()

    x, ctx = dram("x"), dram("ctx_1024")
    wts = {short: dram(name) for short, name in _WEIGHTS.items()}
    out = nc.dram_tensor("out_0_dram", inputs["x"].shape, _mybir.dt.float32, kind="ExternalOutput").ap()
    slots = nc.dram_tensor("slots_dram", (NS * P, REC), _mybir.dt.float32, kind="Internal").ap()
    perceiver_layer(nc, x, ctx, wts, out, slots)
    r = _run(nc, [arrays], core_ids=[0])
    return r.results[0]["out_0_dram"]
```
